# Optimizing a Trainium2 kernel written in Bass

```python
import numpy as np
import jax
import jax.numpy as jnp

def _softmax(x, axis=-1):
    return jax.nn.softmax(x, axis=axis)

def _gelu(x):
    return jax.nn.gelu(x, approximate=True)

def _silu(x):
    return jax.nn.silu(x)

def _sigmoid(x):
    return jax.nn.sigmoid(x)

def _layernorm(x, axis=-1, eps=1e-05):
    m = jnp.mean(x, axis=axis, keepdims=True)
    v = jnp.var(x, axis=axis, keepdims=True)
    return (x - m) / jnp.sqrt(v + eps)

def _scatter_add(tgt, idx, src, axis=0):
    return tgt.at[idx].add(src)

def _segment_sum(src, seg, n):
    return jax.ops.segment_sum(src, seg, n)
kernel_name = 'mk_macaron_d1_jaxref_r8_90f93d'

def setup_inputs(seed: int=0):
    np.random.seed(seed)
    _w = jnp.asarray

    def _L0_attn_setup():
        import jax, jax.numpy as jnp
        import numpy as np
        EPS = 1e-05

        def _proj_ln(x, W, b, g, beta):
            y = jnp.einsum('blc,cd->bld', x, W) + b
            mu = jnp.mean(y, axis=-1, keepdims=True)
            var = jnp.var(y, axis=-1, keepdims=True)
            return (y - mu) * jax.lax.rsqrt(var + EPS) * g + beta
        key = jax.random.key(seed)
        B, L, C, H = (4, 256, 128, 128)
        ks = jax.random.split(key, 7)
        s_in = 1.0 / np.sqrt(C)
        inp = {'input_sequence': jax.random.normal(ks[0], (B, L, C), jnp.float32), 'Wk': jax.random.normal(ks[1], (C, H), jnp.float32) * s_in, 'bk': jnp.zeros((H,), jnp.float32), 'gk': jnp.ones((H,), jnp.float32), 'betak': jnp.zeros((H,), jnp.float32), 'Wq': jax.random.normal(ks[2], (C, H), jnp.float32) * s_in, 'bq': jnp.zeros((H,), jnp.float32), 'gq': jnp.ones((H,), jnp.float32), 'betaq': jnp.zeros((H,), jnp.float32), 'Wv': jax.random.normal(ks[3], (C, C), jnp.float32) * s_in, 'bv': jnp.zeros((C,), jnp.float32), 'gv': jnp.ones((C,), jnp.float32), 'betav': jnp.zeros((C,), jnp.float32)}
        return inp
    _L0_attn_in = _L0_attn_setup()

    def _L0_ffn_setup():
        import jax, jax.numpy as jnp
        import numpy as np
        DIM = 128
        DEPTH = 2
        HEADS = 8
        DIM_HEAD = 64
        WINDOW = 64
        INNER = HEADS * DIM_HEAD
        HID = int(DIM * 4 * 2 / 3)
        B, N = (2, 1024)
        QK_SCALE = 8.0

        def shift_token(t):
            t1, t2 = jnp.split(t, 2, axis=-1)
            t2 = jnp.pad(t2, ((0, 0), (1, 0), (0, 0)))[:, :-1]
            return jnp.concatenate([t1, t2], axis=-1)

        def l2norm(t):
            return t / jnp.clip(jnp.linalg.norm(t, axis=-1, keepdims=True), 1e-12)

        def rotate_half(x):
            x1, x2 = jnp.split(x, 2, axis=-1)
            return jnp.concatenate([-x2, x1], axis=-1)

        def rotary_xpos(q, k):
            n = q.shape[-2]
            half_idx = jnp.arange(0, DIM_HEAD, 2, dtype=jnp.float32)
            inv_freq = 1.0 / 10000.0 ** (half_idx / DIM_HEAD)
            t = jnp.arange(n, dtype=jnp.float32)
            freqs = t[:, None] * inv_freq[None, :]
            freqs = jnp.concatenate([freqs, freqs], axis=-1)
            base = (half_idx + 0.4 * DIM_HEAD) / (1.4 * DIM_HEAD)
            power = (t - n // 2) / float(WINDOW // 2)
            scale = base[None, :] ** power[:, None]
            scale = jnp.concatenate([scale, scale], axis=-1)
            cos, sin = (jnp.cos(freqs), jnp.sin(freqs))
            q = q * cos * scale + rotate_half(q) * sin * scale
            k = k * cos / scale + rotate_half(k) * sin / scale
            return (q, k)

        def local_attention(q, k, v):
            b, h, n, d = q.shape
            w = n // WINDOW
            bq = q.reshape(b, h, w, WINDOW, d) * QK_SCALE
            bk = k.reshape(b, h, w, WINDOW, d)
            bv = v.reshape(b, h, w, WINDOW, d)

            def look_around(t):
                p = jnp.pad(t, ((0, 0), (0, 0), (1, 0), (0, 0), (0, 0)))
                return jnp.concatenate([p[:, :, :w], p[:, :, 1:]], axis=3)
            bk, bv = (look_around(bk), look_around(bv))
            bt = jnp.arange(n).reshape(w, WINDOW)
            btp = jnp.pad(bt, ((1, 0), (0, 0)), constant_values=-1)
            btk = jnp.concatenate([btp[:w], btp[1:]], axis=1)
            sim = jnp.einsum('bhwid,bhwjd->bhwij', bq, bk)
            i = bt[:, :, None]
            j = btk[:, None, :]
            mask = (i < j) | (i > j + WINDOW) | (j == -1)
            sim = jnp.where(mask, -jnp.finfo(sim.dtype).max, sim)
            attn = jax.nn.softmax(sim, axis=-1)
            out = jnp.einsum('bhwij,bhwjd->bhwid', attn, bv)
            return out.reshape(b, h, n, d)

        def _layer(x, wqkv, qs, ksc, wo, lg, lb, w1, b1, w2, b2):
            b, n, _ = x.shape
            h = shift_token(x)
            qkv = h @ wqkv
            q, k, v = jnp.split(qkv, 3, axis=-1)
            to_heads = lambda t: t.reshape(b, n, HEADS, DIM_HEAD).transpose(0, 2, 1, 3)
            q, k, v = (to_heads(q), to_heads(k), to_heads(v))
            q = l2norm(q) * qs
            k = l2norm(k) * ksc
            q, k = rotary_xpos(q, k)
            o = local_attention(q, k, v)
            o = o.transpose(0, 2, 1, 3).reshape(b, n, INNER)
            x = x + o @ wo
            h = shift_token(x)
            mu = h.mean(-1, keepdims=True)
            var = h.var(-1, keepdims=True)
            h = (h - mu) / jnp.sqrt(var + 1e-05) * lg + lb
            h = h @ w1 + b1
            a, g = jnp.split(h, 2, axis=-1)
            h = a * jax.nn.gelu(g, approximate=False)
            x = x + h @ w2 + b2
            return x
        key = jax.random.key(seed)
        ks = jax.random.split(key, 6)
        return {'x': jax.random.normal(ks[0], (B, N, DIM), jnp.float32), 'wqkv': jax.random.normal(ks[1], (DEPTH, DIM, 3 * INNER), jnp.float32) * 0.02, 'q_scale': jnp.ones((DEPTH, DIM_HEAD), jnp.float32), 'k_scale': jnp.ones((DEPTH, DIM_HEAD), jnp.float32), 'wo': jax.random.normal(ks[2], (DEPTH, INNER, DIM), jnp.float32) * 0.02, 'ln_g': jnp.ones((DEPTH, DIM), jnp.float32), 'ln_b': jnp.zeros((DEPTH, DIM), jnp.float32), 'w1': jax.random.normal(ks[3], (DEPTH, DIM, 2 * HID), jnp.float32) * 0.02, 'b1': jnp.zeros((DEPTH, 2 * HID), jnp.float32), 'w2': jax.random.normal(ks[4], (DEPTH, HID, DIM), jnp.float32) * 0.02, 'b2': jnp.zeros((DEPTH, DIM), jnp.float32)}
    _L0_ffn_in = _L0_ffn_setup()
    _d = {'L0_attn_input_sequence': _L0_attn_in['input_sequence'], 'L0_attn_Wk': _L0_attn_in['Wk'], 'L0_attn_bk': _L0_attn_in['bk'], 'L0_attn_gk': _L0_attn_in['gk'], 'L0_attn_betak': _L0_attn_in['betak'], 'L0_attn_Wq': _L0_attn_in['Wq'], 'L0_attn_bq': _L0_attn_in['bq'], 'L0_attn_gq': _L0_attn_in['gq'], 'L0_attn_betaq': _L0_attn_in['betaq'], 'L0_attn_Wv': _L0_attn_in['Wv'], 'L0_attn_bv': _L0_attn_in['bv'], 'L0_attn_gv': _L0_attn_in['gv'], 'L0_attn_betav': _L0_attn_in['betav'], 'L0_ffn_wqkv': _L0_ffn_in['wqkv'], 'L0_ffn_q_scale': _L0_ffn_in['q_scale'], 'L0_ffn_k_scale': _L0_ffn_in['k_scale'], 'L0_ffn_wo': _L0_ffn_in['wo'], 'L0_ffn_ln_g': _L0_ffn_in['ln_g'], 'L0_ffn_ln_b': _L0_ffn_in['ln_b'], 'L0_ffn_w1': _L0_ffn_in['w1'], 'L0_ffn_b1': _L0_ffn_in['b1'], 'L0_ffn_w2': _L0_ffn_in['w2'], 'L0_ffn_b2': _L0_ffn_in['b2']}
    _x0 = _d['L0_attn_input_sequence']
    _d['L0_attn_input_sequence'] = jax.random.normal(jax.random.fold_in(jax.random.key(seed), 1), (4, 1024, 128), dtype=_x0.dtype)
    del _x0
    return _d

def reference(L0_attn_input_sequence, L0_attn_Wk, L0_attn_bk, L0_attn_gk, L0_attn_betak, L0_attn_Wq, L0_attn_bq, L0_attn_gq, L0_attn_betaq, L0_attn_Wv, L0_attn_bv, L0_attn_gv, L0_attn_betav, L0_ffn_wqkv, L0_ffn_q_scale, L0_ffn_k_scale, L0_ffn_wo, L0_ffn_ln_g, L0_ffn_ln_b, L0_ffn_w1, L0_ffn_b1, L0_ffn_w2, L0_ffn_b2):

    def _L0_attn_ref(input_sequence, Wk, bk, gk, betak, Wq, bq, gq, betaq, Wv, bv, gv, betav):
        import jax, jax.numpy as jnp
        import numpy as np
        EPS = 1e-05

        def _proj_ln(x, W, b, g, beta):
            y = jnp.einsum('blc,cd->bld', x, W) + b
            mu = jnp.mean(y, axis=-1, keepdims=True)
            var = jnp.var(y, axis=-1, keepdims=True)
            return (y - mu) * jax.lax.rsqrt(var + EPS) * g + beta
        values = _proj_ln(input_sequence, Wv, bv, gv, betav)
        k = _proj_ln(input_sequence, Wk, bk, gk, betak)
        q = _proj_ln(input_sequence, Wq, bq, gq, betaq)
        scores = jnp.einsum('blc,bLc->blL', k, q)
        attn = jax.nn.softmax(scores, axis=-1)
        out = jnp.einsum('blL,bLc->blc', attn, values)
        return out + input_sequence

    def _L0_ffn_ref(x, wqkv, q_scale, k_scale, wo, ln_g, ln_b, w1, b1, w2, b2):
        import jax, jax.numpy as jnp
        import numpy as np
        DIM = 128
        DEPTH = 2
        HEADS = 8
        DIM_HEAD = 64
        WINDOW = 64
        INNER = HEADS * DIM_HEAD
        HID = int(DIM * 4 * 2 / 3)
        B, N = (2, 1024)
        QK_SCALE = 8.0

        def shift_token(t):
            t1, t2 = jnp.split(t, 2, axis=-1)
            t2 = jnp.pad(t2, ((0, 0), (1, 0), (0, 0)))[:, :-1]
            return jnp.concatenate([t1, t2], axis=-1)

        def l2norm(t):
            return t / jnp.clip(jnp.linalg.norm(t, axis=-1, keepdims=True), 1e-12)

        def rotate_half(x):
            x1, x2 = jnp.split(x, 2, axis=-1)
            return jnp.concatenate([-x2, x1], axis=-1)

        def rotary_xpos(q, k):
            n = q.shape[-2]
            half_idx = jnp.arange(0, DIM_HEAD, 2, dtype=jnp.float32)
            inv_freq = 1.0 / 10000.0 ** (half_idx / DIM_HEAD)
            t = jnp.arange(n, dtype=jnp.float32)
            freqs = t[:, None] * inv_freq[None, :]
            freqs = jnp.concatenate([freqs, freqs], axis=-1)
            base = (half_idx + 0.4 * DIM_HEAD) / (1.4 * DIM_HEAD)
            power = (t - n // 2) / float(WINDOW // 2)
            scale = base[None, :] ** power[:, None]
            scale = jnp.concatenate([scale, scale], axis=-1)
            cos, sin = (jnp.cos(freqs), jnp.sin(freqs))
            q = q * cos * scale + rotate_half(q) * sin * scale
            k = k * cos / scale + rotate_half(k) * sin / scale
            return (q, k)

        def local_attention(q, k, v):
            b, h, n, d = q.shape
            w = n // WINDOW
            bq = q.reshape(b, h, w, WINDOW, d) * QK_SCALE
            bk = k.reshape(b, h, w, WINDOW, d)
            bv = v.reshape(b, h, w, WINDOW, d)

            def look_around(t):
                p = jnp.pad(t, ((0, 0), (0, 0), (1, 0), (0, 0), (0, 0)))
                return jnp.concatenate([p[:, :, :w], p[:, :, 1:]], axis=3)
            bk, bv = (look_around(bk), look_around(bv))
            bt = jnp.arange(n).reshape(w, WINDOW)
            btp = jnp.pad(bt, ((1, 0), (0, 0)), constant_values=-1)
            btk = jnp.concatenate([btp[:w], btp[1:]], axis=1)
            sim = jnp.einsum('bhwid,bhwjd->bhwij', bq, bk)
            i = bt[:, :, None]
            j = btk[:, None, :]
            mask = (i < j) | (i > j + WINDOW) | (j == -1)
            sim = jnp.where(mask, -jnp.finfo(sim.dtype).max, sim)
            attn = jax.nn.softmax(sim, axis=-1)
            out = jnp.einsum('bhwij,bhwjd->bhwid', attn, bv)
            return out.reshape(b, h, n, d)

        def _layer(x, wqkv, qs, ksc, wo, lg, lb, w1, b1, w2, b2):
            b, n, _ = x.shape
            h = shift_token(x)
            qkv = h @ wqkv
            q, k, v = jnp.split(qkv, 3, axis=-1)
            to_heads = lambda t: t.reshape(b, n, HEADS, DIM_HEAD).transpose(0, 2, 1, 3)
            q, k, v = (to_heads(q), to_heads(k), to_heads(v))
            q = l2norm(q) * qs
            k = l2norm(k) * ksc
            q, k = rotary_xpos(q, k)
            o = local_attention(q, k, v)
            o = o.transpose(0, 2, 1, 3).reshape(b, n, INNER)
            x = x + o @ wo
            h = shift_token(x)
            mu = h.mean(-1, keepdims=True)
            var = h.var(-1, keepdims=True)
            h = (h - mu) / jnp.sqrt(var + 1e-05) * lg + lb
            h = h @ w1 + b1
            a, g = jnp.split(h, 2, axis=-1)
            h = a * jax.nn.gelu(g, approximate=False)
            x = x + h @ w2 + b2
            return x
        for l in range(DEPTH):
            x = _layer(x, wqkv[l], q_scale[l], k_scale[l], wo[l], ln_g[l], ln_b[l], w1[l], b1[l], w2[l], b2[l])
        return x
    x = L0_attn_input_sequence
    x = x + 0.5 * _L0_ffn_ref(_layernorm(x, axis=-1), L0_ffn_wqkv, L0_ffn_q_scale, L0_ffn_k_scale, L0_ffn_wo, L0_ffn_ln_g, L0_ffn_ln_b, L0_ffn_w1, L0_ffn_b1, L0_ffn_w2, L0_ffn_b2)
    x = x + _L0_attn_ref(_layernorm(x, axis=-1), L0_attn_Wk, L0_attn_bk, L0_attn_gk, L0_attn_betak, L0_attn_Wq, L0_attn_bq, L0_attn_gq, L0_attn_betaq, L0_attn_Wv, L0_attn_bv, L0_attn_gv, L0_attn_betav)
    x = x + 0.5 * _L0_ffn_ref(_layernorm(x, axis=-1), L0_ffn_wqkv, L0_ffn_q_scale, L0_ffn_k_scale, L0_ffn_wo, L0_ffn_ln_g, L0_ffn_ln_b, L0_ffn_w1, L0_ffn_b1, L0_ffn_w2, L0_ffn_b2)
    return x

_drawn_inputs = setup_inputs


def setup_inputs(seed=0):
    import zlib

    import numpy as np

    out = dict(_drawn_inputs(seed))
    spreads = {'L0_attn_bk': (0.0, 0.1),
     'L0_attn_gk': (1.0, 0.2),
     'L0_attn_betak': (0.0, 0.1),
     'L0_attn_bq': (0.0, 0.285),
     'L0_attn_gq': (1.0, 0.2),
     'L0_attn_betaq': (0.0, 2.0),
     'L0_attn_bv': (0.0, 0.333),
     'L0_attn_gv': (1.0, 0.2),
     'L0_attn_betav': (0.0, 0.367),
     'L0_ffn_q_scale': (1.0, 0.6),
     'L0_ffn_k_scale': (1.0, 0.6),
     'L0_ffn_ln_g': (1.0, 0.6),
     'L0_ffn_ln_b': (0.0, 0.8),
     'L0_ffn_b1': (0.0, 0.8),
     'L0_ffn_b2': (0.0, 0.1)}
    factors = {'L0_ffn_wqkv': 2.78, 'L0_ffn_wo': 2.788, 'L0_ffn_w1': 4.212, 'L0_ffn_w2': 4.195}
    for name, (base, spread) in spreads.items():
        noise = np.random.default_rng([zlib.crc32(name.encode()), seed]).standard_normal(out[name].shape)
        drawn = base * np.exp(spread * noise) if base else spread * noise
        out[name] = jnp.asarray(drawn.astype(out[name].dtype))
    for name, factor in factors.items():
        out[name] = (out[name] * factor).astype(out[name].dtype)
    return out
```

```python
from contextlib import ExitStack

import numpy as np
import concourse.bass as bass
from concourse import mybir

ALU = mybir.AluOpType
ACT = mybir.ActivationFunctionType
AX = mybir.AxisListType.X
F32 = mybir.dt.float32
BF16 = mybir.dt.bfloat16

P = 128
DIM = 128
HEADS = 8
DH = 64
WIN = 64
INNER = HEADS * DH
HID = DIM * 4 * 2 // 3
DEPTH = 2
SEQS = 4
SLEN = 1024
TILES = SLEN // P
ITERS = DEPTH * SEQS
NT = ITERS * TILES
PAIRS = HEADS // 2
CH = [(0, 128), (128, 128), (256, HID - 256)]
EPS = 1e-5
QK_SCALE = float(DH) ** 0.5
HALF = TILES // 2

LOAD, TH, QKV, TQK, ATT, WO, FFN_IN = 0, 1, 2, 3, 4, 5, 6
BURST = TILES + FFN_IN - 1
LAST = (ITERS - 1) * TILES + BURST


class Tile:

    def __init__(self, it, c, stack):
        self.it, self.c = it, c
        self.i = c % TILES
        self.first = stack * NT

    def count(self, back=0, every=1, unit=1):
        c = self.c - back + self.first
        k = (c // every + 1) * unit
        return k if self.it is None else self.it * (TILES // every * unit) + k


    def loads(self):
        k = self.c // TILES
        layer = (k if self.it is None else self.it + k) // SEQS
        return layer + (self.first // NT * DEPTH + 1)


def need(eng, sem, count):
    if not isinstance(count, int) or count > 0:
        eng.wait_ge(sem, count)


def pipeline(eng, step, stack):

    def tile_of(it, g):
        def f(skew):
            c = g - skew
            if it is None and not 0 <= c < NT:
                return None
            return Tile(it, c, stack)
        return f

    def burst_of(it, g):
        if (g - BURST) % TILES or (it is None and g < BURST):
            return None
        n = (g - BURST) // TILES + stack * ITERS
        return n if it is None else it + n

    for g in range(TILES):
        step(tile_of(None, g), burst_of(None, g))
    with eng.Fori(1, ITERS) as it:
        for j in range(TILES):
            step(tile_of(it, j), burst_of(it, j))
    for g in range(NT, LAST + 1):
        step(tile_of(None, g), burst_of(None, g))


def build(nc, x_in, w_attn, b_attn, kq_gain, v_gain, wqkv, qk_gain, wo_in, ln_gb, w1_in, b1_in, w2_in,
          b2_in, rope_in, mask_in, ident_in, out):
    stream = nc.dram_tensor("stream", [DEPTH + 1, SEQS, SLEN + 1, DIM], F32, kind="Internal").ap()
    mid = nc.dram_tensor("mid", [SEQS, SLEN, DIM], F32, kind="Internal").ap()

    with ExitStack() as ctx:
        def sb(name, shape, dt=F32):
            return ctx.enter_context(nc.sbuf_tensor(name, shape, dt))

        def ps(name, cols):
            return ctx.enter_context(nc.psum_tensor(name, [P, cols], F32))

        def sem(name):
            return ctx.enter_context(nc.semaphore(name))

        def sems(name, n):
            return [sem(f"{name}{k}") for k in range(n)]

        ident = sb("ident", [P, P])
        ident_b = sb("ident_b", [P, P], BF16)
        mask_f = sb("mask_f", [P, 2, P])
        mask_b = sb("mask_b", [P, 2, P], BF16)
        zeros = sb("zeros", [P, DIM])
        mhalf = sb("mhalf", [P, 24])
        epsilon = sb("epsilon", [P, 24])
        gain8 = sb("gain8", [P, HEADS])
        w_qkv = sb("w_qkv", [P, 3 * INNER])
        w_o = sb("w_o", [P, PAIRS, DIM])
        w_1raw = sb("w_1raw", [P, DEPTH, 2 * HID])
        w_1all = sb("w_1all", [P, DEPTH, 2 * HID])
        w_1 = sb("w_1", [P, 2 * HID])
        w_2 = sb("w_2", [P, 3, DIM])
        ln_gb_sb = sb("ln_gb_sb", [P, 2, DEPTH])
        b_1raw = sb("b_1raw", [P, DEPTH, 6])
        b_1all = sb("b_1all", [P, DEPTH, 6])
        b_1 = sb("b_1", [P, 6])
        b_2all = sb("b_2all", [P, DEPTH, DIM])
        b_2 = sb("b_2", [P, DIM])
        gains = sb("gains", [P, DEPTH, 2, 2, DH])
        rope_all = sb("rope_all", [P, DEPTH, TILES, 2, 2, DH])
        rope = sb("rope", [P, TILES, 2, 2, DH])
        w_kqv = sb("w_kqv", [P, 3, DIM])
        b_kqv = sb("b_kqv", [P, 3 * DIM])
        kq_gb = sb("kq_gb", [P, 4])
        v_gb = sb("v_gb", [P, 2, DIM])

        x_att = sb("x_att", [P, TILES, DIM])
        x_mid = sb("x_mid", [P, TILES, DIM])
        x_b2 = sb("x_b2", [P, TILES, DIM])
        x_new = sb("x_new", [P, TILES, DIM])
        h = sb("h", [P, 4, DIM])
        hT = sb("hT", [P, 2, P])
        sq = sb("sq", [P, 2 * INNER])
        norm2 = sb("norm2", [P, 2, 2 * HEADS])
        clip2 = sb("clip2", [P, 2, 2 * HEADS])
        rnorm = sb("rnorm", [P, 2, 2 * HEADS])
        qgain = sb("qgain", [P, 2, HEADS])
        rope_c = sb("rope_c", [P, 2 * INNER])
        rope_s = sb("rope_s", [P, 2 * INNER])
        q_r = sb("q_r", [P, 2, INNER])
        k_a = sb("k_a", [P, INNER])
        k_r = sb("k_r", [P, 2, INNER])
        qT = sb("qT", [P, 2, PAIRS, P])
        kT = sb("kT", [P, 2, PAIRS, 2, P])
        v_own = sb("v_own", [P, 4, INNER])
        v_prev = sb("v_prev", [P, 4, INNER])
        top = sb("top", [P, 2, HEADS])
        shift = sb("shift", [P, 2, HEADS])
        probs = sb("probs", [P, 2, HEADS, P])
        psums = sb("psums", [P, 2, HEADS])
        rsums = sb("rsums", [P, 2, HEADS])
        pT = sb("pT", [P, HEADS, P])
        o_n = sb("o_n", [P, INNER])
        oT = sb("oT", [P, PAIRS, P])
        h2 = sb("h2", [P, 4, DIM])
        st2 = sb("st2", [P, 2, 6])
        mv2 = sb("mv2", [P, 2, 2])
        ve2 = sb("ve2", [P, 2, 1])
        rstd2 = sb("rstd2", [P, 2, 1])
        h2n = sb("h2n", [P, 2, DIM])
        h2T = sb("h2T", [P, SLEN])
        gelu = sb("gelu", [P, 2, HALF * P])
        act2 = sb("act2", [P, 2, 3, HALF * P])
        v_g = sb("v_g", [P, TILES, DIM])
        x_2 = sb("x_2", [P, TILES, DIM])
        pT2 = sb("pT2", [P, TILES, P])
        st_g = sb("st_g", [P, 24, 6])
        mv_g = sb("mv_g", [P, 24, 2])
        ve_g = sb("ve_g", [P, 24])
        rs_g = sb("rs_g", [P, 24])
        fence = sb("fence", [P, 1])
        mx_g = sb("mx_g", [P, 2])
        nm_g = sb("nm_g", [P, 2])
        sm_g = sb("sm_g", [P, 2])
        rl_g = sb("rl_g", [P, 2])

        QK = ps("QK", 1024)
        VB = ps("VB", 512)
        SC = ps("SC", 1024)
        TT = ps("TT", 1024)
        OB = ps("OB", 512)

        s_w = sem("s_w")
        s_zero = sem("s_zero")
        s_cast = sem("s_cast")
        s_fold = sem("s_fold")
        s_b1mm = sem("s_b1mm")
        s_b1 = sem("s_b1")
        s_qkvw = sem("s_qkvw")
        s_wow = sem("s_wow")
        s_ffnw = sem("s_ffnw")
        s_rope = sems("s_rope", TILES)
        s_x = sems("s_x", TILES)
        s_h = sems("s_h", 4)
        s_th = sem("s_th")
        s_hT = sem("s_hT")
        s_q = sem("s_q")
        s_k = sem("s_k")
        s_v = sem("s_v")
        s_sq = sem("s_sq")
        s_vown = sem("s_vown")
        s_vlo = sems("s_vlo", 2)
        s_vup = sems("s_vup", 2)
        s_n2 = sem("s_n2")
        s_cl = sem("s_cl")
        s_rn = sem("s_rn")
        s_qg = sem("s_qg")
        s_rot = sem("s_rot")
        s_qr = sem("s_qr")
        s_ka = sem("s_ka")
        s_kr = sem("s_kr")
        s_tqk = sem("s_tqk")
        s_qT = sem("s_qT")
        s_kT = sem("s_kT")
        s_s = sem("s_s")
        s_mx = sem("s_mx")
        s_sh = sem("s_sh")
        s_p = sem("s_p")
        s_tp = sem("s_tp")
        s_pTv = sem("s_pTv")
        s_pTa = sem("s_pTa")
        s_o = sem("s_o")
        s_rsum = sem("s_rsum")
        s_on = sem("s_on")
        s_to = sem("s_to")
        s_oT = sem("s_oT")
        s_y = sem("s_y")
        s_xm = sem("s_xm")
        s_xb2 = sem("s_xb2")
        s_h2 = sems("s_h2", 4)
        s_st2 = sem("s_st2")
        s_mv2 = sem("s_mv2")
        s_ve2 = sem("s_ve2")
        s_rs2 = sem("s_rs2")
        s_h2n = sem("s_h2n")
        s_th2 = sem("s_th2")
        s_h2T = sem("s_h2T")
        s_w1 = sem("s_w1")
        s_gelu = sem("s_gelu")
        s_act2 = sem("s_act2")
        s_w2 = sem("s_w2")
        s_xn = sem("s_xn")
        s_st = sem("s_st")
        g_ld = sem("g_ld")
        g_x1 = sem("g_x1")
        g_st = sem("g_st")
        g_mv = sem("g_mv")
        g_ve = sem("g_ve")
        g_rs = sem("g_rs")
        g_y = sem("g_y")
        g_xy = sem("g_xy")
        g_ty = sem("g_ty")
        g_yT = sem("g_yT")
        g_pr = sem("g_pr")
        g_z = sem("g_z")
        g_zn = sem("g_zn")
        g_vg = sem("g_vg")
        g_tk = sem("g_tk")
        g_kT = sem("g_kT")
        g_s = sem("g_s")
        g_mx = sem("g_mx")
        g_nm = sem("g_nm")
        g_p = sem("g_p")
        g_tp = sem("g_tp")
        g_pTv = sem("g_pTv")
        g_pTa = sem("g_pTa")
        g_o = sem("g_o")
        g_rl = sem("g_rl")
        g_x2 = sem("g_x2")
        g_sto = sem("g_sto")

        block = ctx.enter_context(nc.Block())

        def banks(k):
            src = TT if k % 2 == 0 else QK
            return src[:, 0:512], src[:, 512:1024]

        def qk(ap):
            return ap.rearrange("p (t h d) -> p t h d", t=2, d=DH)

        def rows(ap):
            return ap.rearrange("(t p) c -> p t c", p=P)

        def stack_done(eng, stack):
            eng.wait_ge(s_st, (stack + 1) * ITERS * 32 + 16)

        @block.sync
        def _(sp):
            for dst, src in ((ident[:], ident_in), (mask_f[:], mask_in), (rope_all[:, 0], rope_in),
                             (rope_all[:, 1], rope_in), (w_1raw[:], w1_in.rearrange("l c n -> c l n")),
                             (w_kqv[:], w_attn), (kq_gb[:], kq_gain), (ln_gb_sb[:], ln_gb),
                             (b_kqv[:], b_attn.partition_broadcast(P)),
                             (v_gb[:], v_gain.partition_broadcast(P)),
                             (b_2all[:], b2_in.partition_broadcast(P)),
                             (gains[:, :, :, 0, :], qk_gain.partition_broadcast(P)),
                             (gains[:, :, :, 1, 0:32], qk_gain[:, :, 32:64].partition_broadcast(P)),
                             (gains[:, :, :, 1, 32:64], qk_gain[:, :, 0:32].partition_broadcast(P))):
                sp.dma_start(dst, src).then_inc(s_w, 16)
            sp.dma_start(b_1raw[:], b1_in).then_inc(s_w, 16)
            sp.wait_ge(s_zero, ZEROED)
            sp.dma_start(stream[:, :, 0, :].rearrange("l s c -> (l s) c"), zeros[0:(DEPTH + 1) * SEQS, :]).then_inc(s_st, 16)

            for s in range(SEQS):
                need(sp, g_y, s)
                sp.dma_start(x_att[:], rows(x_in[s])).then_inc(g_ld, 16)
                sp.wait_ge(g_y, s + 1)
                sp.dma_start(rows(stream[0, s, 1:, :]), x_new[:]).then_inc(g_sto, 16)
            sp.wait_ge(g_sto, 16 * SEQS)
            sp.wait_ge(s_w, N_CONST)
            sp.wait_ge(s_st, 16)
            sp.wait_ge(s_fold, 3)
            sp.wait_ge(s_b1, 1)

            def load_rope(l, i):
                sp.dma_start(rope[:, i], rope_all[:, l, i]).then_inc(s_rope[i], 16)

            def load_ffn(l):
                sp.dma_start(w_1[:], w_1all[:, l]).then_inc(s_ffnw, 16)
                sp.dma_start(b_1[:], b_1all[:, l]).then_inc(s_ffnw, 16)
                sp.dma_start(b_2[:], b_2all[:, l]).then_inc(s_ffnw, 16)
                for c, (at, n) in enumerate(CH):
                    sp.dma_start(w_2[0:n, c, :], w2_in[l, at:at + n, :]).then_inc(s_ffnw, 16)

            def load_qkv(l):
                sp.dma_start(w_qkv[:], wqkv[l]).then_inc(s_qkvw, 16)

            def load_wo(l):
                sp.dma_start(w_o[:], wo_in[l].rearrange("(c p) n -> p c n", p=P)).then_inc(s_wow, 16)

            def loads(t, l, s):
                i, k = t.i, t.i % 4
                base = P * i
                sp.dma_start(x_att[:, i, :], stream[l, s, base + 1:base + 1 + P, :]).then_inc(s_x[i], 16)
                sp.dma_start(h[:, k, 0:64], stream[l, s, base + 1:base + 1 + P, 0:64]).then_inc(s_h[k], 16)
                sp.dma_start(h[:, k, 64:128], stream[l, s, base:base + P, 64:128]).then_inc(s_h[k], 16)

            def moves(tile):
                if t := tile(QKV):
                    a, k = t.i % 2, t.i % 4
                    need(sp, s_vown, t.count())
                    sp.dma_start(v_prev[0:64, k, :], v_own[0:64, k, :]).then_inc(s_vlo[a], 16)
                    sp.dma_start(v_prev[64:128, (k + 1) % 4, :], v_own[64:128, k, :]).then_inc(s_vup[a], 16)
                if t := tile(WO):
                    i, k = t.i, t.i % 4
                    need(sp, s_xm, t.count())
                    sp.dma_start(h2[:, k, 0:64], x_mid[:, i, 0:64]).then_inc(s_h2[k], 16)
                    sp.dma_start(h2[1:128, k, 64:128], x_mid[0:127, i, 64:128]).then_inc(s_h2[k], 16)
                    before = x_mid[127:128, i - 1, 64:128] if i else zeros[0:1, 0:64]
                    sp.dma_start(h2[0:1, k, 64:128], before).then_inc(s_h2[k], 16)

            def store(l, s, n):
                for half in range(2):
                    need(sp, s_xn, n * 2 + (half + 1))
                    a, b = half * HALF, (half + 1) * HALF
                    sp.dma_start(rows(stream[l + 1, s, 1 + a * P:1 + b * P, :]), x_new[:, a:b, :]).then_inc(s_st, 16)

            def stack(k):
                first = k * ITERS

                def iteration(it, c, l, s, lb, sb_, at=(), after_burst=None):
                    for j in range(TILES):
                        def tile(skew):
                            n = j - skew + c
                            return Tile(it, n, k) if it is not None or 0 <= n < NT else None
                        if l is not None:
                            if not isinstance(l, int) or l > 0:
                                if j == 0:
                                    need(sp, s_st, (first - 1 + (c // TILES if it is None else it)) * 32 + 16)
                            loads(tile(0), l, s)
                        for when, do in at:
                            if when == j:
                                do()
                        moves(tile)
                        if j == BURST - TILES and lb is not None:
                            store(lb, sb_, (c // TILES if it is None else it) - 1 + first)
                            if after_burst:
                                after_burst()

                def wait_tile(s_, n, unit=1):
                    need(sp, s_, (n + k * NT + 1) * unit)

                load_qkv(0)
                for i in range(TILES):
                    load_rope(0, i)
                load_wo(0)
                load_ffn(0)
                iteration(None, 0, 0, 0, None, None)
                with sp.Fori(1, SEQS - 1) as it:
                    iteration(it, 0, 0, it, 0, it - 1)
                m = (SEQS - 1) * TILES

                def rope_after(i):
                    def do():
                        wait_tile(s_rot, m + i)
                        load_rope(1, i)
                    return do

                iteration(None, m, 0, SEQS - 1, 0, SEQS - 2,
                          [(i + 3, rope_after(i)) for i in range(TILES - 3)])

                def after_qkv():
                    wait_tile(s_v, m + TILES - 1)
                    load_qkv(1)

                def after_wo():
                    wait_tile(s_y, m + TILES - 1)
                    load_wo(1)

                iteration(None, m + TILES, 1, 0, 0, SEQS - 1,
                          [(0, rope_after(5)), (1, rope_after(6)), (2, after_qkv), (2, rope_after(7)), (5, after_wo)],
                          lambda: load_ffn(1))
                with sp.Fori(SEQS + 1, ITERS) as it:
                    iteration(it, 0, 1, it - SEQS, 1, it - SEQS - 1)
                for g in range(NT, LAST + 1):
                    moves(lambda skew: Tile(None, g - skew, k) if 0 <= g - skew < NT else None)
                store(1, SEQS - 1, first + ITERS - 1)

            stack(0)
            stack_done(sp, 0)
            with sp.Fori(0, SEQS) as s:
                need(sp, g_sto, (s * 2 + SEQS) * 16)
                sp.dma_start(x_att[:], rows(x_in[s])).then_inc(g_ld, 16)
                sp.dma_start(x_b2[:], rows(stream[DEPTH, s, 1:, :])).then_inc(g_ld, 16)
                need(sp, g_x2, (s + 1) * TILES)
                sp.dma_start(rows(mid[s]), x_2[:]).then_inc(g_sto, 16)
                need(sp, g_y, SEQS + (s + 1) * 2)
                sp.dma_start(rows(stream[0, s, 1:, :]), x_new[:]).then_inc(g_sto, 16)
            need(sp, g_sto, SEQS * 3 * 16)
            stack(1)
            stack_done(sp, 1)
            for s in range(SEQS):
                if s:
                    need(sp, g_x2, SEQS * TILES + s)
                sp.dma_start(x_att[:], rows(mid[s])).then_inc(g_ld, 16)
                sp.dma_start(x_b2[:], rows(stream[DEPTH, s, 1:, :])).then_inc(g_ld, 16)
                need(sp, g_x2, SEQS * TILES + s + 1)
                sp.dma_start(rows(out[s]), x_new[:]).then_inc(g_sto, 16)
                need(sp, g_sto, (SEQS * 3 + s + 1) * 16)

        @block.tensor
        def _(pe):
            mm = nc.tensor.matmul

            def transpose(dst, src):
                return nc.tensor.transpose(dst, src, ident[:])

            pe.wait_ge(s_w, N_CONST)
            pe.wait_ge(s_cast, 2)
            for l in range(DEPTH):
                for g in range(2):
                    for c, (at, n) in enumerate(CH):
                        k = (l * 2 + g) * 3 + c
                        last = mm(VB[0:n, k:k + 1], w_1raw[:, l, g * HID + at:g * HID + at + n],
                                  ln_gb_sb[:, 1, l:l + 1], start=True, stop=True)
            last.then_inc(s_b1mm, 1)
            pe.wait_ge(s_b1, 1)

            def step(stack):
                def f(tile, burst):
                    if t := tile(QKV):
                        i, b = t.i, t.i % 2
                        if i == 0:
                            pe.wait_ge(s_qkvw, t.loads() * 16)
                        pe.wait_ge(s_hT, t.count())
                        need(pe, s_rot, t.count(back=1))
                        need(pe, s_sq, t.count(back=1))
                        for m, signal in ((0, s_q), (1, s_k)):
                            mm(QK[:, m * 512:m * 512 + 512], hT[:, b, :], w_qkv[:, m * 512:m * 512 + 512],
                               start=True, stop=True).then_inc(signal, 1)
                        if t2 := tile(FFN_IN + 1):
                            pe.wait_ge(s_h2T, t2.count())
                        mm(VB[:], hT[:, b, :], w_qkv[:, 1024:1536], start=True, stop=True).then_inc(s_v, 1)
                    if t := tile(WO):
                        if t.i == 0:
                            pe.wait_ge(s_wow, t.loads() * 16)
                        pe.wait_ge(s_oT, t.count())
                        for c in range(PAIRS):
                            last = mm(OB[:, 0:DIM], oT[:, c, :], w_o[:, c, :], start=(c == 0), stop=(c == PAIRS - 1))
                        last.then_inc(s_y, 1)
                    if t := tile(ATT):
                        b = t.i % 2
                        pe.wait_ge(s_p, t.count())
                        pe.wait_ge(s_qT, t.count())
                        pe.wait_ge(s_kT, t.count())
                        for hd in range(HEADS):
                            last = transpose(TT[:, hd * P:hd * P + P], probs[:, b, hd, :])
                        last.then_inc(s_tp, 1)
                    if t := tile(TH):
                        pe.wait_ge(s_h[t.i % 4], t.count(every=4, unit=32))
                        need(pe, s_vown, t.count(back=1))
                        need(pe, s_hT, t.count(back=1))
                        transpose(VB[:, 0:P], h[:, t.i % 4, :]).then_inc(s_th, 1)
                    if t := tile(FFN_IN):
                        pe.wait_ge(s_h2n, t.count())
                        if t2 := tile(QKV):
                            pe.wait_ge(s_vown, t2.count())
                        else:
                            pe.wait_ge(s_h2T, t.count(back=1))
                        transpose(VB[:, P:2 * P], h2n[:, t.i % 2, :]).then_inc(s_th2, 1)
                    if t := tile(ATT):
                        b = t.i % 2
                        pe.wait_ge(s_pTv, t.count())
                        pe.wait_ge(s_pTa, t.count())
                        need(pe, s_xm, t.count(back=1))
                        pe.wait_ge(s_vlo[b], t.count(every=2, unit=16))
                        if t.it is not None or t.c > 0:
                            pe.wait_ge(s_vup[1 - b], t.count(back=1, every=2, unit=16))
                        for w, v in ((0, v_prev), (1, v_own)):
                            for hd in range(HEADS):
                                last = mm(OB[64 * w:64 * w + 64, hd * DH:hd * DH + DH],
                                          pT[:, hd, 64 * w:64 * w + 64], v[:, t.i % 4, hd * DH:hd * DH + DH],
                                          start=True, stop=True)
                        last.then_inc(s_o, 1)
                    if t := tile(TQK):
                        b = t.i % 2
                        pe.wait_ge(s_qr, t.count())
                        pe.wait_ge(s_kr, t.count())
                        for m, src in ((0, q_r), (1, k_r)):
                            for c in range(PAIRS):
                                last = transpose(TT[:, m * 512 + c * P:m * 512 + c * P + P], src[:, b, c * P:c * P + P])
                        last.then_inc(s_tqk, 1)
                    if t := tile(ATT):
                        pe.wait_ge(s_on, t.count())
                        for c in range(PAIRS):
                            last = transpose(OB[:, c * P:c * P + P], o_n[:, c * P:c * P + P])
                        last.then_inc(s_to, 1)
                    if t := tile(TQK):
                        i, b = t.i, t.i % 2
                        need(pe, s_p, t.count(back=1))
                        m = 1 if i == 0 else 0
                        for bank in range(2):
                            mm(SC[:, bank * 512:bank * 512 + 512], ident_b[:],
                               mask_b[:, m:m + 1, :].to_broadcast([P, 4, P]), start=True, stop=False,
                               skip_group_check=True)
                        pe.wait_ge(s_qT, t.count())
                        pe.wait_ge(s_kT, t.count())
                        sc = SC[:, :].rearrange("q (c e b k) -> q c e b k", c=PAIRS, e=2, b=2)
                        for c in range(PAIRS):
                            last = mm(sc[:, c, :, 0, :], qT[:, b, c, :], kT[:, b, c, :, 0:64],
                                      start=False, stop=True, skip_group_check=True)
                        for c in range(PAIRS):
                            if i:
                                last = mm(sc[0:64, c, :, 1, :], qT[:, b, c, 0:64], kT[:, 1 - b, c, :, 64:128],
                                          start=False, stop=True, skip_group_check=True)
                        for c in range(PAIRS):
                            last = mm(sc[64:128, c, :, 1, :], qT[:, b, c, 64:128], kT[:, b, c, :, 64:128],
                                      start=False, stop=True, skip_group_check=True)
                        last.then_inc(s_s, 1)
                    if burst is not None:
                        ffn(tile, burst)
                return f

            def ffn(tile, n):
                last_in = tile(FFN_IN)
                pe.wait_ge(s_h2T, last_in.count())
                pe.wait_ge(s_ffnw, last_in.loads() * 96)
                if t := tile(QKV):
                    pe.wait_ge(s_rot, t.count())
                    pe.wait_ge(s_sq, t.count())
                if t := tile(TQK):
                    pe.wait_ge(s_kT, t.count())

                def w1_pair(k):
                    half, c = divmod(k, 3)
                    at, m = CH[c]
                    a, g = banks(k)
                    if k >= 2:
                        pe.wait_ge(s_act2, n * 6 + (k - 1))
                    rhs = h2T[:, half * 512:half * 512 + 512]
                    mm(g[0:m], w_1[:, HID + at:HID + at + m], rhs, start=True, stop=True)
                    mm(a[0:m], w_1[:, at:at + m], rhs, start=True, stop=True).then_inc(s_w1, 1)

                def w2_half(half):
                    dst = VB if half == 0 else OB
                    pe.wait_ge(s_act2, n * 6 + (3 * half + 3))
                    if half == 0:
                        if t := tile(TH):
                            pe.wait_ge(s_hT, t.count())
                    elif t := tile(ATT):
                        pe.wait_ge(s_oT, t.count())
                    for q in range(HALF):
                        for c, (at, m) in enumerate(CH):
                            last = mm(dst[:, q * DIM:q * DIM + DIM], act2[0:m, half, c, q * P:q * P + P],
                                      w_2[0:m, c, :], start=(c == 0), stop=(c == 2))
                    last.then_inc(s_w2, 1)

                for k in range(4):
                    w1_pair(k)
                w2_half(0)
                w1_pair(4)
                w1_pair(5)
                w2_half(1)
                pe.wait_ge(s_xn, n * 2 + 2)

            pipeline(pe, step(0), 0)
            stack_done(pe, 0)

            with pe.Fori(0, SEQS) as s:
                pe.wait_ge(g_y, s * 2 + (SEQS + 1))
                for i in range(TILES):
                    last = transpose(TT[:, i * P:i * P + P], x_new[:, i, :])
                last.then_inc(g_ty, 1)
                pe.wait_ge(g_yT, s + 1)
                for i in range(TILES):
                    if i >= 2:
                        pe.wait_ge(g_z, s * TILES + (i - 1))
                    mm(QK[:, i % 2 * 512:i % 2 * 512 + 384], h2T[:, i * P:i * P + P],
                       w_kqv[:, :, :].rearrange("p a b -> p (a b)"), start=True, stop=True).then_inc(g_pr, 1)
                zn = act2[:].rearrange("p a b c -> p (a b c)").rearrange("p (i m) -> p i m", i=TILES)
                pe.wait_ge(g_zn, s + 1)
                for m, dst in ((0, TT), (1, SC)):
                    for i in range(TILES):
                        last = transpose(dst[:, i * P:i * P + P], zn[:, i, m * DIM:m * DIM + DIM])
                    last.then_inc(g_tk, 1)
                pe.wait_ge(g_kT, s * 2 + 2)
                for i in range(TILES + 1):
                    if i < TILES:
                        dst = QK if i % 2 else SC
                        if i >= 2:
                            pe.wait_ge(g_p, s * TILES + (i - 1))
                        for m in range(2):
                            last = mm(dst[:, m * 512:m * 512 + 512], rope_c[:, i * P:i * P + P],
                                      rope_s[:, m * 512:m * 512 + 512], start=True, stop=True)
                        last.then_inc(g_s, 1)
                    if i:
                        k = i - 1
                        pe.wait_ge(g_p, s * TILES + (k + 1))
                        if k:
                            pe.wait_ge(g_pTv, s * TILES + k)
                            pe.wait_ge(g_pTa, s * TILES + k)
                        for m in range(TILES):
                            last = transpose(TT[:, m * P:m * P + P], probs[:, k % 2, m, :])
                        last.then_inc(g_tp, 1)
                        pe.wait_ge(g_pTv, s * TILES + (k + 1))
                        pe.wait_ge(g_pTa, s * TILES + (k + 1))
                        if k >= 2:
                            pe.wait_ge(g_x2, s * TILES + (k - 1))
                        if k == 0:
                            pe.wait_ge(g_vg, s * 2 + 2)
                        dst = OB if k % 2 else VB
                        src = pT2 if k % 2 else pT
                        for m in range(TILES):
                            last = mm(dst[:, 0:DIM], src[:, m, :], v_g[:, m, :], start=(m == 0), stop=(m == TILES - 1))
                        last.then_inc(g_o, 1)
                pe.wait_ge(g_x2, s * TILES + TILES)

            pipeline(pe, step(1), 1)

        @block.vector
        def _(dve):
            v = nc.vector
            v.memset(zeros[:], 0.0).then_inc(s_zero, 1)
            v.memset(v_prev[:], 0.0).then_inc(s_zero, 1)
            v.memset(kT[:], 0.0).then_inc(s_zero, 1)
            v.memset(b_1all[:], 0.0).then_inc(s_zero, 1)
            v.memset(mhalf[:], -0.5).then_inc(s_zero, 1)
            v.memset(epsilon[:], EPS).then_inc(s_zero, 1)
            v.memset(gain8[:], QK_SCALE).then_inc(s_zero, 1)
            dve.wait_ge(s_w, N_CONST)
            v.tensor_copy(ident_b[:], ident[:]).then_inc(s_cast, 1)
            v.tensor_copy(mask_b[:], mask_f[:]).then_inc(s_cast, 1)
            for l in range(DEPTH):
                v.tensor_tensor(rope_all[:, l].rearrange("p t a b d -> p t (a b d)"),
                                rope_all[:, l].rearrange("p t a b d -> p t (a b d)"),
                                gains[:, l].rearrange("p a b d -> p (a b d)").unsqueeze(1).to_broadcast([P, TILES, 4 * DH]),
                                ALU.mult).then_inc(s_fold, 1)
            dve.wait_ge(s_b1mm, 1)
            dve.wait_ge(s_zero, ZEROED)
            for l in range(DEPTH):
                for c in range(6):
                    n = CH[c % 3][1]
                    k = l * 6 + c
                    last = v.tensor_tensor(b_1all[0:n, l, c:c + 1], VB[0:n, k:k + 1], b_1raw[0:n, l, c:c + 1], ALU.add)
            last.then_inc(s_b1, 1)

            def stats(src, n, slot0=0):
                for k in range(n):
                    last = v.bn_stats(st_g[:, slot0 + k, :], src(k))
                return last

            def stats_fence(n):
                dve.wait_ge(g_st, n * 2 - 1)
                v.tensor_copy(fence[:], zeros[:, 0:1]).then_inc(g_st, 1)

            def aggregate(n):
                for k in range(n):
                    last = v.bn_aggr(mv_g[:, k, :], st_g[:, k, :])
                return last

            def layer_norm(src, dst, n_st, n_rs):
                stats(lambda k: src[:, k, :], TILES).then_inc(g_st, 1)
                stats_fence(n_st)
                aggregate(TILES).then_inc(g_mv, 1)
                dve.wait_ge(g_rs, n_rs)
                for k in range(TILES):
                    last = v.tensor_scalar(dst[:, k, :], src[:, k, :], mv_g[:, k, 0:1], rs_g[:, k:k + 1],
                                           ALU.subtract, ALU.mult)
                return last

            for s in range(SEQS):
                dve.wait_ge(g_ld, 16 * (s + 1))
                need(dve, g_sto, 16 * s)
                layer_norm(x_att, x_new, s + 1, s + 1).then_inc(g_y, 1)

            def step(tile, burst):
                if t := tile(FFN_IN):
                    b, k = t.i % 2, t.i % 4
                    dve.wait_ge(s_h2[k], t.count(every=4, unit=48))
                    v.bn_stats(st2[:, b, :], h2[:, k, :]).then_inc(s_st2, 1)
                if t := tile(ATT):
                    b = t.i % 2
                    dve.wait_ge(s_s, t.count())
                    v.tensor_reduce(top[:, b, :], SC[:, :].rearrange("q (h k) -> q h k", h=HEADS), AX, ALU.max).then_inc(s_mx, 1)
                    dve.wait_ge(s_mx, t.count())
                    dve.wait_ge(s_qg, t.count())
                    if t2 := tile(FFN_IN):
                        dve.wait_ge(s_st2, t2.count())
                    v.scalar_tensor_tensor(out=shift[:, b, :], in0=top[:, b, :], scalar=-1.0, in1=qgain[:, b, :],
                                           op0=ALU.mult, op1=ALU.mult).then_inc(s_sh, 1)
                if t := tile(FFN_IN):
                    b = t.i % 2
                    if not tile(ATT):
                        dve.wait_ge(s_st2, t.count())
                    v.bn_aggr(mv2[:, b, :], st2[:, b, :]).then_inc(s_mv2, 1)
                if t := tile(QKV):
                    i = t.i
                    dve.wait_ge(s_rope[i], t.loads() * 16)
                    need(dve, s_qr, t.count(back=1))
                    need(dve, s_ka, t.count(back=1))
                    for m, signal in ((0, s_q), (1, s_k)):
                        dve.wait_ge(signal, t.count())
                        src = qk(QK[:, :])[:, m]
                        v.tensor_tensor(qk(rope_c[:])[:, m], src,
                                        rope[:, i, m, 0:1, :].to_broadcast([P, HEADS, DH]), ALU.mult)
                        sin = rope[:, i, m, 1:2, :]
                        for half in range(2):
                            a, o = 32 * half, 32 * (1 - half)
                            last = v.tensor_tensor(qk(rope_s[:])[:, m, :, a:a + 32], src[:, :, o:o + 32],
                                                   sin[:, :, a:a + 32].to_broadcast([P, HEADS, 32]), ALU.mult)
                    last.then_inc(s_rot, 1)
                if t := tile(FFN_IN):
                    b, k = t.i % 2, t.i % 4
                    dve.wait_ge(s_rs2, t.count())
                    need(dve, s_th2, t.count(back=2))
                    v.tensor_scalar(h2n[:, b, :], h2[:, k, :], mv2[:, b, 0:1], rstd2[:, b, :],
                                    ALU.subtract, ALU.mult).then_inc(s_h2n, 1)
                if t := tile(WO):
                    i, b = t.i, t.i % 2
                    dve.wait_ge(s_y, t.count())
                    dve.wait_ge(s_x[i], t.count(every=TILES, unit=16))
                    need(dve, s_xb2, t.count(back=2))
                    v.tensor_tensor(x_mid[:, i, :], OB[:, 0:DIM], x_att[:, i, :], ALU.add).then_inc(s_xm, 1)
                if t := tile(ATT):
                    dve.wait_ge(s_tp, t.count())
                    need(dve, s_o, t.count(back=1))
                    v.tensor_copy(pT[:, 0:4, :], TT[:, 0:512].rearrange("k (h q) -> k h q", h=4)).then_inc(s_pTv, 1)
                if t := tile(QKV):
                    b = t.i % 2
                    dve.wait_ge(s_sq, t.count())
                    need(dve, s_rn, t.count(back=2))
                    v.tensor_reduce(norm2[:, b, :], sq[:].rearrange("p (h d) -> p h d", d=DH), AX, ALU.add).then_inc(s_n2, 1)
                    dve.wait_ge(s_n2, t.count())
                    v.tensor_scalar(clip2[:, b, :], norm2[:, b, :], 1e-24, None, ALU.max).then_inc(s_cl, 1)
                if t := tile(ATT):
                    b = t.i % 2
                    v.reciprocal(rsums[:, b, :], psums[:, b, :]).then_inc(s_rsum, 1)
                    dve.wait_ge(s_rsum, t.count())
                    dve.wait_ge(s_o, t.count())
                    need(dve, s_to, t.count(back=1))
                    v.tensor_tensor(o_n[:].rearrange("q (h d) -> q h d", h=HEADS),
                                    OB[:, :].rearrange("q (h d) -> q h d", h=HEADS),
                                    rsums[:, b, :].unsqueeze(2).to_broadcast([P, HEADS, DH]), ALU.mult).then_inc(s_on, 1)
                if burst is not None:
                    n = burst
                    for k in range(6):
                        half, c = divmod(k, 3)
                        m = CH[c][1]
                        dve.wait_ge(s_gelu, n * 6 + (k + 1))
                        v.scalar_tensor_tensor(out=act2[0:m, half, c, :], in0=banks(k)[0][0:m], scalar=b_1[0:m, c:c + 1],
                                               in1=gelu[0:m, k % 2, :], op0=ALU.add, op1=ALU.mult).then_inc(s_act2, 1)
                        if k == 3 or k == 5:
                            half = k // 4
                            dve.wait_ge(s_w2, n * 2 + (half + 1))
                            if half == 0:
                                dve.wait_ge(s_xb2, tile(FFN_IN).count())
                                dve.wait_ge(s_st, n * 32 + 16)
                            src = (VB if half == 0 else OB)[:, :].rearrange("p (t c) -> p t c", t=HALF)
                            v.tensor_tensor(x_new[:, half * HALF:half * HALF + HALF, :], src,
                                            x_b2[:, half * HALF:half * HALF + HALF, :], ALU.add).then_inc(s_xn, 1)

            pipeline(dve, step, 0)
            stack_done(dve, 0)

            with dve.Fori(0, SEQS) as s:
                dve.wait_ge(g_ld, s * 32 + (SEQS * 16 + 32))
                dve.wait_ge(g_sto, (s * 2 + SEQS) * 16)
                v.scalar_tensor_tensor(out=x_mid[:].rearrange("p t c -> p (t c)"), in0=x_b2[:].rearrange("p t c -> p (t c)"),
                                       scalar=0.5, in1=x_att[:].rearrange("p t c -> p (t c)"),
                                       op0=ALU.mult, op1=ALU.add).then_inc(g_x1, 1)
                dve.wait_ge(g_x1, s + 1)
                layer_norm(x_mid, x_new, s * 3 + (SEQS + 1), s * 3 + (SEQS + 1)).then_inc(g_y, 1)
                z = act2[:].rearrange("p a b c -> p (a b c)").rearrange("p (i m) -> p i m", i=TILES)
                for i in range(TILES):
                    dve.wait_ge(g_pr, s * TILES + (i + 1))
                    v.tensor_tensor(z[:, i, :], QK[:, i % 2 * 512:i % 2 * 512 + 384], b_kqv[:], ALU.add).then_inc(g_z, 1)
                dve.wait_ge(g_z, s * TILES + TILES)
                stats(lambda k: z[:, k % 8, k // 8 * DIM:k // 8 * DIM + DIM], 24).then_inc(g_st, 1)
                stats_fence(s * 3 + (SEQS + 2))
                aggregate(24).then_inc(g_mv, 1)
                dve.wait_ge(g_rs, s * 3 + (SEQS + 2))
                for k in range(24):
                    zz = z[:, k % 8, k // 8 * DIM:k // 8 * DIM + DIM]
                    last = v.tensor_scalar(zz, zz, mv_g[:, k, 0:1], rs_g[:, k:k + 1], ALU.subtract, ALU.mult)
                last.then_inc(g_zn, 1)
                for i in range(TILES + 1):
                    if i < TILES:
                        b = i % 2
                        dve.wait_ge(g_s, s * TILES + (i + 1))
                        v.tensor_reduce(mx_g[:, b:b + 1], (QK if b else SC)[:, :], AX, ALU.max).then_inc(g_mx, 1)
                        dve.wait_ge(g_mx, s * TILES + (i + 1))
                        v.tensor_scalar(nm_g[:, b:b + 1], mx_g[:, b:b + 1], -1.0, None, ALU.mult).then_inc(g_nm, 1)
                    if i:
                        k = i - 1
                        b = k % 2
                        dve.wait_ge(g_tp, s * TILES + (k + 1))
                        if k >= 2:
                            dve.wait_ge(g_o, s * TILES + (k - 1))
                        v.tensor_copy((pT2 if b else pT)[:, 0:4, :],
                                      TT[:, 0:512].rearrange("k (h q) -> k h q", h=4)).then_inc(g_pTv, 1)
                        v.reciprocal(rl_g[:, b:b + 1], sm_g[:, b:b + 1]).then_inc(g_rl, 1)
                        dve.wait_ge(g_rl, s * TILES + (k + 1))
                        dve.wait_ge(g_o, s * TILES + (k + 1))
                        if k == 0:
                            dve.wait_ge(g_xy, s + 1)
                        v.scalar_tensor_tensor(out=x_2[:, k, :], in0=(OB if b else VB)[:, 0:DIM], scalar=rl_g[:, b:b + 1],
                                               in1=sq[:, k * DIM:k * DIM + DIM], op0=ALU.mult, op1=ALU.add).then_inc(g_x2, 1)
                dve.wait_ge(g_x2, s * TILES + TILES)
                layer_norm(x_2, x_new, s * 3 + (SEQS + 3), s * 3 + (SEQS + 3)).then_inc(g_y, 1)

            pipeline(dve, step, 1)
            for s in range(SEQS):
                dve.wait_ge(g_ld, SEQS * 16 + SEQS * 32 + (s + 1) * 32)
                dve.wait_ge(g_sto, (SEQS * 3 + s) * 16)
                v.scalar_tensor_tensor(out=x_new[:].rearrange("p t c -> p (t c)"), in0=x_b2[:].rearrange("p t c -> p (t c)"),
                                       scalar=0.5, in1=x_att[:].rearrange("p t c -> p (t c)"),
                                       op0=ALU.mult, op1=ALU.add).then_inc(g_x2, 1)

        @block.scalar
        def _(act):
            def copy(dst, src):
                return nc.scalar.activation(dst, src, ACT.Copy)

            def step(tile, burst):
                if t := tile(ATT):
                    b = t.i % 2
                    act.wait_ge(s_sh, t.count())
                    need(act, s_tp, t.count(back=2))
                    need(act, s_rsum, t.count(back=2))
                    for hd in range(HEADS):
                        last = nc.scalar.activation(probs[:, b, hd, :], SC[:, hd * P:hd * P + P], ACT.Exp,
                                                    bias=shift[:, b, hd:hd + 1], scale=qgain[:, b, hd:hd + 1],
                                                    accum_out=psums[:, b, hd:hd + 1])
                    last.then_inc(s_p, 1)
                if t := tile(QKV):
                    b = t.i % 2
                    act.wait_ge(s_v, t.count())
                    need(act, s_o, t.count(back=3))
                    if t.it is not None or t.c >= 2:
                        act.wait_ge(s_vlo[b], t.count(back=2, every=2, unit=16))
                        act.wait_ge(s_vup[b], t.count(back=2, every=2, unit=16))
                    copy(v_own[:, t.i % 4, :], VB[:]).then_inc(s_vown, 1)
                    act.wait_ge(s_k, t.count())
                    need(act, s_n2, t.count(back=1))
                    act.wait_ge(s_rot, t.count())
                    nc.scalar.activation(sq[:], QK[:], ACT.Square).then_inc(s_sq, 1)
                if t := tile(ATT):
                    act.wait_ge(s_tp, t.count())
                    need(act, s_o, t.count(back=1))
                    copy(pT[:, 4:8, :], TT[:, 512:1024].rearrange("k (h q) -> k h q", h=4)).then_inc(s_pTa, 1)
                if t := tile(TH):
                    act.wait_ge(s_th, t.count())
                    if t2 := tile(FFN_IN):
                        act.wait_ge(s_th2, t2.count())
                    need(act, s_v, t.count(back=2))
                    copy(hT[:, t.i % 2, :], VB[:, 0:P]).then_inc(s_hT, 1)
                if t := tile(FFN_IN):
                    act.wait_ge(s_th2, t.count())
                    copy(h2T[:, t.i * P:t.i * P + P], VB[:, P:2 * P]).then_inc(s_h2T, 1)
                if t := tile(TQK):
                    b = t.i % 2
                    act.wait_ge(s_tqk, t.count())
                    need(act, s_s, t.count(back=1))
                    copy(qT[:, b], TT[:, 0:512].rearrange("d (c t) -> d c t", c=PAIRS)).then_inc(s_qT, 1)
                    for e in range(2):
                        last = copy(kT[64 * e:64 * e + 64, b, :, e, :],
                                    TT[64 * e:64 * e + 64, 512:1024].rearrange("d (c t) -> d c t", c=PAIRS))
                    last.then_inc(s_kT, 1)
                if t := tile(ATT):
                    act.wait_ge(s_to, t.count())
                    need(act, s_y, t.count(back=1))
                    copy(oT[:], OB[:].rearrange("d (c t) -> d c t", c=PAIRS)).then_inc(s_oT, 1)
                if burst is not None:
                    n = burst
                    for k in range(6):
                        c = k % 3
                        m = CH[c][1]
                        act.wait_ge(s_w1, n * 6 + (k + 1))
                        if k >= 2:
                            act.wait_ge(s_act2, n * 6 + (k - 1))
                        nc.scalar.activation(gelu[0:m, k % 2, :], banks(k)[1][0:m], ACT.Gelu,
                                             bias=b_1[0:m, 3 + c:4 + c]).then_inc(s_gelu, 1)

            act.wait_ge(s_zero, ZEROED)
            pipeline(act, step, 0)
            stack_done(act, 0)

            with act.Fori(0, SEQS) as s:
                act.wait_ge(g_ty, s + 1)
                copy(h2T[:], TT[:]).then_inc(g_yT, 1)
                for m, src, dst in ((0, TT, rope_c), (1, SC, rope_s)):
                    act.wait_ge(g_tk, s * 2 + (m + 1))
                    nc.scalar.activation(dst[:], src[:], ACT.Identity, bias=kq_gb[:, 2 * m + 1:2 * m + 2],
                                         scale=kq_gb[:, 2 * m:2 * m + 1]).then_inc(g_kT, 1)
                for i in range(TILES + 1):
                    if i < TILES:
                        b = i % 2
                        act.wait_ge(g_nm, s * TILES + (i + 1))
                        if i >= 2:
                            act.wait_ge(g_tp, s * TILES + (i - 1))
                            act.wait_ge(g_rl, s * TILES + (i - 1))
                        nc.scalar.activation(probs[:, b].rearrange("p a b -> p (a b)"), (QK if b else SC)[:], ACT.Exp,
                                             bias=nm_g[:, b:b + 1], accum_out=sm_g[:, b:b + 1]).then_inc(g_p, 1)
                    if i:
                        k = i - 1
                        b = k % 2
                        act.wait_ge(g_tp, s * TILES + (k + 1))
                        if k >= 2:
                            act.wait_ge(g_o, s * TILES + (k - 1))
                        copy((pT2 if b else pT)[:, 4:8, :],
                             TT[:, 512:1024].rearrange("k (h q) -> k h q", h=4)).then_inc(g_pTa, 1)

            pipeline(act, step, 1)

        @block.gpsimd
        def _(pool):
            g = nc.gpsimd
            pool.wait_ge(s_w, N_CONST)
            for l in range(DEPTH):
                last = g.tensor_scalar(w_1all[:, l, :], w_1raw[:, l, :], ln_gb_sb[:, 0, l:l + 1], None, ALU.mult)
            last.then_inc(s_fold, 1)
            pool.wait_ge(s_zero, ZEROED)

            def rstd(n, mv_count, ve_count):
                need(pool, g_mv, mv_count)
                g.tensor_tensor(ve_g[:, 0:n], mv_g[:, 0:n, 1], epsilon[:, 0:n], ALU.add).then_inc(g_ve, 1)
                pool.wait_ge(g_ve, ve_count)
                g.tensor_tensor(rs_g[:, 0:n], ve_g[:, 0:n], mhalf[:, 0:n], ALU.pow).then_inc(g_rs, 1)

            for s in range(SEQS):
                rstd(TILES, s + 1, s + 1)

            def step(tile, burst):
                if t := tile(FFN_IN):
                    i, b = t.i, t.i % 2
                    if i == 0:
                        pool.wait_ge(s_ffnw, t.loads() * 96)
                        k = t.count(back=TILES, every=TILES, unit=2)
                        need(pool, s_xn, k)
                    pool.wait_ge(s_xm, t.count())
                    g.tensor_tensor(x_b2[:, i, :], x_mid[:, i, :], b_2[:], ALU.add).then_inc(s_xb2, 1)
                    need(pool, s_mv2, t.count())
                    g.tensor_tensor(ve2[:, b, :], mv2[:, b, 1:2], epsilon[:, 0:1], ALU.add).then_inc(s_ve2, 1)
                    pool.wait_ge(s_ve2, t.count())
                    g.tensor_tensor(rstd2[:, b, :], ve2[:, b, :], mhalf[:, 0:1], ALU.pow).then_inc(s_rs2, 1)
                if t := tile(QKV):
                    b = t.i % 2
                    pool.wait_ge(s_rot, t.count())
                    need(pool, s_tqk, t.count(back=2))
                    g.tensor_tensor(q_r[:, b, :], rope_c[:, 0:512], rope_s[:, 0:512], ALU.add).then_inc(s_qr, 1)
                    need(pool, s_kr, t.count(back=1))
                    g.tensor_tensor(k_a[:], rope_c[:, 512:1024], rope_s[:, 512:1024], ALU.add).then_inc(s_ka, 1)
                    pool.wait_ge(s_cl, t.count())
                    g.tensor_tensor(rnorm[:, b, :], clip2[:, b, :], mhalf[:, 0:16], ALU.pow).then_inc(s_rn, 1)
                    pool.wait_ge(s_rn, t.count())
                    pool.wait_ge(s_ka, t.count())
                    g.tensor_tensor(k_r[:, b, :].rearrange("p (h d) -> p h d", h=HEADS),
                                    k_a[:].rearrange("p (h d) -> p h d", h=HEADS),
                                    rnorm[:, b, 8:16].unsqueeze(2).to_broadcast([P, HEADS, DH]), ALU.mult).then_inc(s_kr, 1)
                    need(pool, s_p, t.count(back=2))
                    g.tensor_tensor(qgain[:, b, :], rnorm[:, b, 0:8], gain8[:], ALU.mult).then_inc(s_qg, 1)

            pipeline(pool, step, 0)
            stack_done(pool, 0)

            with pool.Fori(0, SEQS) as s:
                rstd(TILES, s * 3 + (SEQS + 1), s * 3 + (SEQS + 1))
                pool.wait_ge(g_y, s * 2 + (SEQS + 1))
                g.tensor_tensor(sq[:], x_mid[:].rearrange("p t c -> p (t c)"), x_new[:].rearrange("p t c -> p (t c)"),
                                ALU.add).then_inc(g_xy, 1)
                rstd(24, s * 3 + (SEQS + 2), s * 3 + (SEQS + 2))
                pool.wait_ge(g_zn, s + 1)
                z = act2[:].rearrange("p a b c -> p (a b c)").rearrange("p (i m) -> p i m", i=TILES)
                vz = z[:, :, 2 * DIM:3 * DIM]
                g.tensor_tensor(x_b2[:], vz, v_gb[:, 0:1, :].to_broadcast([P, TILES, DIM]), ALU.mult).then_inc(g_vg, 1)
                pool.wait_ge(g_vg, s * 2 + 1)
                g.tensor_tensor(v_g[:], x_b2[:], v_gb[:, 1:2, :].to_broadcast([P, TILES, DIM]), ALU.add).then_inc(g_vg, 1)
                rstd(TILES, s * 3 + (SEQS + 3), s * 3 + (SEQS + 3))

            pipeline(pool, step, 1)


ZEROED = 7
N_CONST = 15 * 16


def tables():
    f = np.float32
    half_idx = np.arange(0, DH, 2, dtype=f)
    inv_freq = (f(1.0) / np.power(f(10000.0), half_idx / f(DH))).astype(f)
    t = np.arange(SLEN, dtype=f)
    ang = (t[:, None] * inv_freq[None, :]).astype(f)
    base = ((half_idx + f(0.4 * DH)) / f(1.4 * DH)).astype(f)
    power = ((t - f(SLEN // 2)) / f(WIN // 2)).astype(f)
    scale = np.power(base[None, :], power[:, None]).astype(f)
    cos, sin = np.cos(ang), np.sin(ang)
    rope = np.zeros((SLEN, 2, 2, DH), f)
    for m, sc in ((0, scale), (1, f(1.0) / scale)):
        rope[:, m, 0, :32] = rope[:, m, 0, 32:] = cos * sc
        rope[:, m, 1, :32] = -sin * sc
        rope[:, m, 1, 32:] = sin * sc
    rope = rope.reshape(TILES, P, 2, 2, DH).transpose(1, 0, 2, 3, 4)
    r = np.arange(WIN)[:, None]
    c = np.arange(WIN)[None, :]
    own, prev = (c <= r), (c >= r)
    allowed = np.zeros((2, P, P), bool)
    allowed[:, :64, :64] = own
    allowed[:, 64:, :64] = prev
    allowed[0, :64, 64:] = prev
    allowed[:, 64:, 64:] = own
    mask = np.where(allowed, 0.0, -1e30).astype(f).transpose(1, 0, 2)
    return (np.ascontiguousarray(rope), np.ascontiguousarray(mask), np.eye(P, dtype=f))


def kernel(**inputs):
    import concourse.bacc as bacc
    from concourse.bass_utils import run_bass_kernel_spmd

    a = {k: np.asarray(v) for k, v in inputs.items()}
    A, L = "L0_attn_", "L0_ffn_"
    rope, mask, ident = tables()
    b1 = np.zeros((DEPTH, 2, 3 * P), a[L + "b1"].dtype)
    b1[:, :, :HID] = a[L + "b1"].reshape(DEPTH, 2, HID)
    b1 = b1.reshape(DEPTH, 6, P).transpose(2, 0, 1)
    arrays = {
        "x_in": a[A + "input_sequence"],
        "w_attn": np.stack([a[A + "Wk"], a[A + "Wq"], a[A + "Wv"]], axis=1),
        "b_attn": np.concatenate([a[A + "bk"], a[A + "bq"], a[A + "bv"]]),
        "kq_gain": np.stack([a[A + "gk"], a[A + "betak"], a[A + "gq"], a[A + "betaq"]], axis=1),
        "v_gain": np.stack([a[A + "gv"], a[A + "betav"]]),
        "wqkv": a[L + "wqkv"],
        "qk_gain": np.stack([a[L + "q_scale"], a[L + "k_scale"]], axis=1),
        "wo_in": a[L + "wo"],
        "ln_gb": np.stack([a[L + "ln_g"].T, a[L + "ln_b"].T], axis=1),
        "w1_in": a[L + "w1"], "b1_in": b1, "w2_in": a[L + "w2"], "b2_in": a[L + "b2"],
        "rope_in": rope, "mask_in": mask, "ident_in": ident,
    }
    arrays = {k: np.ascontiguousarray(v) for k, v in arrays.items()}
    nc = bacc.Bacc("TRN2", target_bir_lowering=False, num_devices=1)
    args = [nc.dram_tensor(k, v.shape, mybir.dt.from_np(v.dtype), kind="ExternalInput").ap() for k, v in arrays.items()]
    out = nc.dram_tensor("out", [SEQS, SLEN, DIM], F32, kind="ExternalOutput").ap()
    build(nc, *args, out)
    r = run_bass_kernel_spmd(nc, [arrays], core_ids=[0])
    return r.results[0]["out"]
```

```python
from contextlib import ExitStack

import numpy as np
import concourse.bass as bass
from concourse import mybir

ALU = mybir.AluOpType
ACT = mybir.ActivationFunctionType
AX = mybir.AxisListType.X
F32 = mybir.dt.float32
BF16 = mybir.dt.bfloat16

P = 128
DIM = 128
HEADS = 8
DH = 64
WIN = 64
INNER = HEADS * DH
HID = DIM * 4 * 2 // 3
DEPTH = 2
SEQS = 4
SLEN = 1024
TILES = SLEN // P
ITERS = DEPTH * SEQS
NT = ITERS * TILES
PAIRS = HEADS // 2
CH = [(0, 128), (128, 128), (256, HID - 256)]
EPS = 1e-5
QK_SCALE = float(DH) ** 0.5
HALF = TILES // 2

LOAD, TH, QKV, TQK, ATT, WO, FFN_IN = 0, 1, 2, 3, 4, 5, 6
BURST = TILES + FFN_IN - 1
LAST = (ITERS - 1) * TILES + BURST

KQV, LN_OUT, LN_IN = 0, 3 * TILES, 4 * TILES
SLOTS = 5 * TILES


class Tile:

    def __init__(self, it, c, stack):
        self.it, self.c = it, c
        self.i = c % TILES
        self.first = stack * NT

    def count(self, back=0, every=1, unit=1):
        c = self.c - back + self.first
        k = (c // every + 1) * unit
        return k if self.it is None else self.it * (TILES // every * unit) + k


    def loads(self):
        k = self.c // TILES
        layer = (k if self.it is None else self.it + k) // SEQS
        return layer + (self.first // NT * DEPTH + 1)


def need(eng, sem, count):
    if not isinstance(count, int) or count > 0:
        eng.wait_ge(sem, count)


def pipeline(eng, step, stack):

    def tile_of(it, g):
        def f(skew):
            c = g - skew
            if it is None and not 0 <= c < NT:
                return None
            return Tile(it, c, stack)
        return f

    def burst_of(it, g):
        if (g - BURST) % TILES or (it is None and g < BURST):
            return None
        n = (g - BURST) // TILES + stack * ITERS
        return n if it is None else it + n

    for g in range(TILES):
        step(tile_of(None, g), burst_of(None, g), None)
    with eng.Fori(1, ITERS) as it:
        for j in range(TILES):
            step(tile_of(it, j), burst_of(it, j), burst_of(it, j - 1))
    for g in range(NT, LAST + 2):
        step(tile_of(None, g), burst_of(None, g), burst_of(None, g - 1))


def build(nc, x_in, w_attn, b_attn, kq_gain, v_gain, wqkv, qk_gain, wo_in, ln_gb, w1_in, b1_in, w2_in,
          b2_in, rope_in, mask_in, ident_in, out):
    stream = nc.dram_tensor("stream", [DEPTH + 1, SEQS, SLEN + 1, DIM], F32, kind="Internal").ap()
    mid = nc.dram_tensor("mid", [SEQS, SLEN, DIM], F32, kind="Internal").ap()

    with ExitStack() as ctx:
        def sb(name, shape, dt=F32):
            return ctx.enter_context(nc.sbuf_tensor(name, shape, dt))

        def ps(name, cols):
            return ctx.enter_context(nc.psum_tensor(name, [P, cols], F32))

        def sem(name):
            return ctx.enter_context(nc.semaphore(name))

        def sems(name, n):
            return [sem(f"{name}{k}") for k in range(n)]

        ident = sb("ident", [P, P])
        ident_b = sb("ident_b", [P, P], BF16)
        mask_f = sb("mask_f", [P, 2, P])
        mask_b = sb("mask_b", [P, 2, P], BF16)
        zeros = sb("zeros", [P, DIM])
        mhalf = sb("mhalf", [P, 24])
        epsilon = sb("epsilon", [P, 24])
        w_qkv = sb("w_qkv", [P, 3 * INNER])
        w_o = sb("w_o", [P, PAIRS, DIM])
        w_1raw = sb("w_1raw", [P, DEPTH, 2 * HID])
        w_1all = sb("w_1all", [P, DEPTH, 2 * HID])
        w_1 = sb("w_1", [P, 2 * HID])
        w_2 = sb("w_2", [P, 3, DIM])
        ln_gb_sb = sb("ln_gb_sb", [P, 2, DEPTH])
        b_1raw = sb("b_1raw", [P, DEPTH, 6])
        b_1all = sb("b_1all", [P, DEPTH, 6])
        b_1 = sb("b_1", [P, 6])
        b_2all = sb("b_2all", [P, DEPTH, DIM])
        b_2 = sb("b_2", [P, DIM])
        gains = sb("gains", [P, DEPTH, 2, 2, DH])
        rope_all = sb("rope_all", [P, DEPTH, TILES, 2, 2, DH])
        rope = sb("rope", [P, TILES, 2, 2, DH])
        w_kqv = sb("w_kqv", [P, 3, DIM])
        b_kqv = sb("b_kqv", [P, 3 * DIM])
        kq_gb = sb("kq_gb", [P, 4])
        v_gb = sb("v_gb", [P, 2, DIM])

        x_att = sb("x_att", [P, TILES, DIM])
        x_mid = sb("x_mid", [P, TILES, DIM])
        x_b2 = sb("x_b2", [P, TILES, DIM])
        x_new = sb("x_new", [P, TILES, DIM])
        h = sb("h", [P, 4, DIM])
        hT = sb("hT", [P, 2, P])
        sq = sb("sq", [P, 2 * INNER])
        norm2 = sb("norm2", [P, 2, 2 * HEADS])
        clip2 = sb("clip2", [P, 2, 2 * HEADS])
        rnorm = sb("rnorm", [P, 2, HEADS])
        qgain = sb("qgain", [P, 2, HEADS])
        rope_c = sb("rope_c", [P, 2 * INNER])
        rope_s = sb("rope_s", [P, 2 * INNER])
        q_r = sb("q_r", [P, 2, INNER])
        k_a = sb("k_a", [P, INNER])
        k_r = sb("k_r", [P, 2, INNER])
        qT = sb("qT", [P, 2, PAIRS, P])
        kT = sb("kT", [P, 2, PAIRS, 2, P])
        v_own = sb("v_own", [P, 4, INNER])
        v_prev = sb("v_prev", [P, 4, INNER])
        top = sb("top", [P, 2, HEADS])
        shift = sb("shift", [P, 2, HEADS])
        probs = sb("probs", [P, 2, HEADS, P])
        psums = sb("psums", [P, 2, HEADS])
        rsums = sb("rsums", [P, 2, HEADS])
        pT = sb("pT", [P, HEADS, P])
        o_n = sb("o_n", [P, INNER])
        oT = sb("oT", [P, PAIRS, P])
        h2 = sb("h2", [P, 4, DIM])
        st2 = sb("st2", [P, 2, 6])
        mv2 = sb("mv2", [P, 2, 2])
        ve2 = sb("ve2", [P, 2, 1])
        rstd2 = sb("rstd2", [P, 2, 1])
        h2n = sb("h2n", [P, 2, DIM])
        h2T = sb("h2T", [P, SLEN])
        gelu = sb("gelu", [P, 2, HALF * P])
        act2 = sb("act2", [P, 2, 3, HALF * P])
        v_g = sb("v_g", [P, TILES, DIM])
        x_2 = sb("x_2", [P, TILES, DIM])
        pT2 = sb("pT2", [P, TILES, P])
        st_g = sb("st_g", [P, SLOTS, 6])
        mv_g = sb("mv_g", [P, SLOTS, 2])
        ve_g = sb("ve_g", [P, SLOTS])
        rs_g = sb("rs_g", [P, SLOTS])
        fence = sb("fence", [P, 1])
        mx_g = sb("mx_g", [P, 2])
        nm_g = sb("nm_g", [P, 2])
        sm_g = sb("sm_g", [P, 2])
        rl_g = sb("rl_g", [P, 2])

        QK = ps("QK", 1024)
        VB = ps("VB", 512)
        SC = ps("SC", 1024)
        TT = ps("TT", 1024)
        OB = ps("OB", 512)

        s_w = sem("s_w")
        s_zero = sem("s_zero")
        s_cast = sem("s_cast")
        s_fold = sem("s_fold")
        s_b1mm = sem("s_b1mm")
        s_b1 = sem("s_b1")
        s_qkvw = sem("s_qkvw")
        s_wow = sem("s_wow")
        s_ffnw = sem("s_ffnw")
        s_rope = sems("s_rope", TILES)
        s_x = sems("s_x", TILES)
        s_h = sems("s_h", 4)
        s_th = sem("s_th")
        s_hT = sem("s_hT")
        s_q = sem("s_q")
        s_k = sem("s_k")
        s_v = sem("s_v")
        s_sq = sem("s_sq")
        s_vown = sem("s_vown")
        s_vlo = sems("s_vlo", 2)
        s_vup = sems("s_vup", 2)
        s_n2 = sem("s_n2")
        s_cl = sem("s_cl")
        s_rn = sem("s_rn")
        s_qg = sem("s_qg")
        s_rot = sem("s_rot")
        s_qr = sem("s_qr")
        s_ka = sem("s_ka")
        s_kr = sem("s_kr")
        s_tqk = sem("s_tqk")
        s_qT = sem("s_qT")
        s_kT = sem("s_kT")
        s_s = sem("s_s")
        s_mx = sem("s_mx")
        s_sh = sem("s_sh")
        s_p = sem("s_p")
        s_tp = sem("s_tp")
        s_pTv = sem("s_pTv")
        s_pTa = sem("s_pTa")
        s_o = sem("s_o")
        s_rsum = sem("s_rsum")
        s_on = sem("s_on")
        s_to = sem("s_to")
        s_oT = sem("s_oT")
        s_y = sem("s_y")
        s_xm = sem("s_xm")
        s_xb2 = sem("s_xb2")
        s_h2 = sems("s_h2", 4)
        s_st2 = sem("s_st2")
        s_mv2 = sem("s_mv2")
        s_ve2 = sem("s_ve2")
        s_rs2 = sem("s_rs2")
        s_h2n = sem("s_h2n")
        s_th2 = sem("s_th2")
        s_h2T = sem("s_h2T")
        s_w1 = sem("s_w1")
        s_gelu = sem("s_gelu")
        s_act2 = sem("s_act2")
        s_w2 = sem("s_w2")
        s_xn = sem("s_xn")
        s_st = sem("s_st")
        g_in = sems("g_in", SEQS)
        g_fin = sems("g_fin", SEQS)
        g_ld = sem("g_ld")
        g_x1 = sem("g_x1")
        g_st = sem("g_st")
        g_mv = sem("g_mv")
        g_ve = sem("g_ve")
        g_rs = sem("g_rs")
        g_y = sem("g_y")
        g_xy = sem("g_xy")
        g_ty = sem("g_ty")
        g_yT = sem("g_yT")
        g_pr = sem("g_pr")
        g_z = sem("g_z")
        g_zn = sem("g_zn")
        g_vg = sem("g_vg")
        g_tk = sem("g_tk")
        g_kT = sem("g_kT")
        g_s = sem("g_s")
        g_mx = sem("g_mx")
        g_nm = sem("g_nm")
        g_p = sem("g_p")
        g_tp = sem("g_tp")
        g_pTv = sem("g_pTv")
        g_pTa = sem("g_pTa")
        g_o = sem("g_o")
        g_rl = sem("g_rl")
        g_x2 = sem("g_x2")
        g_sto = sem("g_sto")

        block = ctx.enter_context(nc.Block())

        arrived = (x_att, x_mid, x_b2, x_2)
        kept = (v_g, x_2, pT2, pT)
        half_step = (x_att, x_mid, x_b2, sq)

        y_in = gelu[:].rearrange("p a (t c) -> p (a t) c", c=DIM)

        def flat(buf):
            return buf[:].rearrange("p t c -> p (t c)") if len(buf.shape) == 3 else buf[:]

        def tokens(buf):
            return buf[:] if len(buf.shape) == 3 else buf[:].rearrange("p (t c) -> p t c", t=TILES)

        def banks(k):
            src = TT if k % 2 == 0 else QK
            return src[:, 0:512], src[:, 512:1024]

        def qk(ap):
            return ap.rearrange("p (t h d) -> p t h d", t=2, d=DH)

        def rows(ap):
            return ap.rearrange("(t p) c -> p t c", p=P)

        def stack_done(eng, stack):
            eng.wait_ge(s_st, (stack + 1) * ITERS * 32 + 16)

        @block.sync
        def _(sp):
            for s in range(SEQS):
                sp.dma_start(arrived[s][:], rows(x_in[s])).then_inc(g_in[s], 16)
            for dst, src in ((ident[:], ident_in), (mask_f[:], mask_in), (rope_all[:, 0], rope_in),
                             (rope_all[:, 1], rope_in), (w_1raw[:], w1_in.rearrange("l c n -> c l n")),
                             (w_kqv[:], w_attn), (kq_gb[:], kq_gain), (ln_gb_sb[:], ln_gb),
                             (b_kqv[:], b_attn.partition_broadcast(P)),
                             (v_gb[:], v_gain.partition_broadcast(P)),
                             (b_2all[:], b2_in.partition_broadcast(P)),
                             (gains[:, :, :, 0, :], qk_gain.partition_broadcast(P)),
                             (gains[:, :, :, 1, 0:32], qk_gain[:, :, 32:64].partition_broadcast(P)),
                             (gains[:, :, :, 1, 32:64], qk_gain[:, :, 0:32].partition_broadcast(P))):
                sp.dma_start(dst, src).then_inc(s_w, 16)
            sp.dma_start(b_1raw[:], b1_in).then_inc(s_w, 16)
            sp.wait_ge(s_zero, ZEROED)
            sp.dma_start(stream[:, :, 0, :].rearrange("l s c -> (l s) c"), zeros[0:(DEPTH + 1) * SEQS, :]).then_inc(s_st, 16)

            def load_rope(l, i):
                sp.dma_start(rope[:, i], rope_all[:, l, i]).then_inc(s_rope[i], 16)

            def load_ffn(l):
                sp.dma_start(w_1[:], w_1all[:, l]).then_inc(s_ffnw, 16)
                sp.dma_start(b_1[:], b_1all[:, l]).then_inc(s_ffnw, 16)
                sp.dma_start(b_2[:], b_2all[:, l]).then_inc(s_ffnw, 16)
                for c, (at, n) in enumerate(CH):
                    sp.dma_start(w_2[0:n, c, :], w2_in[l, at:at + n, :]).then_inc(s_ffnw, 16)

            def load_qkv(l):
                sp.dma_start(w_qkv[:], wqkv[l]).then_inc(s_qkvw, 16)

            def load_wo(l):
                sp.dma_start(w_o[:], wo_in[l].rearrange("(c p) n -> p c n", p=P)).then_inc(s_wow, 16)

            def loads(t, l, s):
                i, k = t.i, t.i % 4
                base = P * i
                sp.dma_start(x_att[:, i, :], stream[l, s, base + 1:base + 1 + P, :]).then_inc(s_x[i], 16)
                sp.dma_start(h[:, k, 0:64], stream[l, s, base + 1:base + 1 + P, 0:64]).then_inc(s_h[k], 16)
                sp.dma_start(h[:, k, 64:128], stream[l, s, base:base + P, 64:128]).then_inc(s_h[k], 16)

            def moves(tile):
                if t := tile(QKV):
                    a, k = t.i % 2, t.i % 4
                    need(sp, s_vown, t.count())
                    sp.dma_start(v_prev[0:64, k, :], v_own[0:64, k, :]).then_inc(s_vlo[a], 16)
                    sp.dma_start(v_prev[64:128, (k + 1) % 4, :], v_own[64:128, k, :]).then_inc(s_vup[a], 16)
                if t := tile(WO):
                    i, k = t.i, t.i % 4
                    need(sp, s_xm, t.count())
                    sp.dma_start(h2[:, k, 0:64], x_mid[:, i, 0:64]).then_inc(s_h2[k], 16)
                    sp.dma_start(h2[1:128, k, 64:128], x_mid[0:127, i, 64:128]).then_inc(s_h2[k], 16)
                    before = x_mid[127:128, i - 1, 64:128] if i else zeros[0:1, 0:64]
                    sp.dma_start(h2[0:1, k, 64:128], before).then_inc(s_h2[k], 16)

            def store(l, s, n):
                for half in range(2):
                    need(sp, s_xn, n * 2 + (half + 1))
                    a, b = half * HALF, (half + 1) * HALF
                    sp.dma_start(rows(stream[l + 1, s, 1 + a * P:1 + b * P, :]), x_new[:, a:b, :]).then_inc(s_st, 16)

            def stack(k):
                first = k * ITERS

                def iteration(it, c, l, s, lb, sb_, at=(), after_burst=None):
                    for j in range(TILES):
                        def tile(skew):
                            n = j - skew + c
                            return Tile(it, n, k) if it is not None or 0 <= n < NT else None
                        if l is not None:
                            if not isinstance(l, int) or l > 0:
                                if j == 0:
                                    need(sp, s_st, (first - 1 + (c // TILES if it is None else it)) * 32 + 16)
                            loads(tile(0), l, s)
                        for when, do in at:
                            if when == j:
                                do()
                        moves(tile)
                        if j == BURST - TILES and lb is not None:
                            store(lb, sb_, (c // TILES if it is None else it) - 1 + first)
                            if after_burst:
                                after_burst()

                def wait_tile(s_, n, unit=1):
                    need(sp, s_, (n + k * NT + 1) * unit)

                load_qkv(0)
                load_wo(0)
                if k == 0:
                    for s in range(SEQS):
                        sp.wait_ge(g_y, s + 1)
                        sp.dma_start(rows(stream[0, s, 1:, :]), arrived[s][:]).then_inc(g_sto, 16)
                    sp.wait_ge(s_w, N_CONST)
                    sp.wait_ge(s_fold, 3)
                    sp.wait_ge(s_b1, 1)
                for i in range(TILES):
                    load_rope(0, i)
                load_ffn(0)
                if k == 0:
                    sp.wait_ge(g_sto, 16 * SEQS)
                    sp.wait_ge(s_st, 16)
                iteration(None, 0, 0, 0, None, None)
                with sp.Fori(1, SEQS - 1) as it:
                    iteration(it, 0, 0, it, 0, it - 1)
                m = (SEQS - 1) * TILES

                def rope_after(i):
                    def do():
                        wait_tile(s_rot, m + i)
                        load_rope(1, i)
                    return do

                iteration(None, m, 0, SEQS - 1, 0, SEQS - 2,
                          [(i + 3, rope_after(i)) for i in range(TILES - 3)])

                def after_qkv():
                    wait_tile(s_v, m + TILES - 1)
                    load_qkv(1)

                def after_wo():
                    wait_tile(s_y, m + TILES - 1)
                    load_wo(1)

                iteration(None, m + TILES, 1, 0, 0, SEQS - 1,
                          [(0, rope_after(5)), (1, rope_after(6)), (2, after_qkv), (2, rope_after(7)), (5, after_wo)],
                          lambda: load_ffn(1))
                with sp.Fori(SEQS + 1, ITERS) as it:
                    iteration(it, 0, 1, it - SEQS, 1, it - SEQS - 1)
                for g in range(NT, LAST + 1):
                    moves(lambda skew: Tile(None, g - skew, k) if 0 <= g - skew < NT else None)
                store(1, SEQS - 1, first + ITERS - 1)

            stack(0)
            stack_done(sp, 0)

            def attention_loads(s):
                sp.dma_start(x_att[:], rows(x_in[s])).then_inc(g_ld, 16)
                sp.dma_start(x_b2[:], rows(stream[DEPTH, s, 1:, :])).then_inc(g_ld, 16)

            def attention(s, more):
                if more:
                    sp.wait_ge(g_x1, s + 1)
                    attention_loads(s + 1)
                sp.wait_ge(g_x2, (s + 1) * TILES)
                sp.dma_start(rows(mid[s]), x_2[:]).then_inc(g_sto, 16)
                sp.wait_ge(g_y, s * 2 + (SEQS + 2))
                sp.dma_start(rows(stream[0, s, 1:, :]), x_new[:]).then_inc(g_sto, 16)

            attention_loads(0)
            with sp.Fori(0, SEQS - 1) as s:
                attention(s, True)
            attention(SEQS - 1, False)
            sp.wait_ge(g_sto, SEQS * 3 * 16)
            for s in range(SEQS - 1):
                sp.dma_start(tokens(kept[s]), rows(mid[s])).then_inc(g_fin[s], 16)
            stack(1)
            stack_done(sp, 1)
            sp.dma_start(tokens(kept[SEQS - 1]), rows(mid[SEQS - 1])).then_inc(g_fin[SEQS - 1], 16)
            for s in range(SEQS):
                sp.dma_start(tokens(half_step[s]), rows(stream[DEPTH, s, 1:, :])).then_inc(g_fin[s], 16)
            for s in range(SEQS):
                sp.wait_ge(g_x2, SEQS * TILES + s + 1)
                sp.dma_start(rows(out[s]), tokens(kept[s])).then_inc(g_sto, 16)
            sp.wait_ge(g_sto, SEQS * 4 * 16)

        @block.tensor
        def _(pe):
            mm = nc.tensor.matmul

            def transpose(dst, src):
                return nc.tensor.transpose(dst, src, ident[:])

            pe.wait_ge(s_w, N_CONST)
            pe.wait_ge(s_cast, 2)
            for l in range(DEPTH):
                for g in range(2):
                    for c, (at, n) in enumerate(CH):
                        k = (l * 2 + g) * 3 + c
                        last = mm(VB[0:n, k:k + 1], w_1raw[:, l, g * HID + at:g * HID + at + n],
                                  ln_gb_sb[:, 1, l:l + 1], start=True, stop=True)
            last.then_inc(s_b1mm, 1)
            pe.wait_ge(s_b1, 1)

            def probs_transposed(t, half):
                pe.wait_ge(s_p, t.count(unit=2) + (half - 1))
                for hd in range(4 * half, 4 * half + 4):
                    last = transpose(TT[:, hd * P:hd * P + P], probs[:, t.i % 2, hd, :])
                last.then_inc(s_tp, 1)

            def masked(t, bank):
                m = 1 if t.i == 0 else 0
                mm(SC[:, bank * 512:bank * 512 + 512], ident_b[:],
                   mask_b[:, m:m + 1, :].to_broadcast([P, 4, P]), start=True, stop=False,
                   skip_group_check=True)

            def step(stack):
                def f(tile, burst, before):
                    if t := tile(QKV):
                        i, b = t.i, t.i % 2
                        if i == 0:
                            pe.wait_ge(s_qkvw, t.loads() * 16)
                        pe.wait_ge(s_hT, t.count())
                        if tile(TQK + 1):
                            pe.wait_ge(s_qT, t.count(back=2))
                            pe.wait_ge(s_kT, t.count(back=2))
                        else:
                            need(pe, s_rot, t.count(back=1))
                            need(pe, s_sq, t.count(back=1))
                        for m, signal in ((0, s_q), (1, s_k)):
                            mm(QK[:, m * 512:m * 512 + 512], hT[:, b, :], w_qkv[:, m * 512:m * 512 + 512],
                               start=True, stop=True).then_inc(signal, 1)
                        if t2 := tile(FFN_IN + 1):
                            pe.wait_ge(s_h2T, t2.count())
                        if before is not None:
                            pe.wait_ge(s_xn, before * 2 + 1)
                        mm(VB[:], hT[:, b, :], w_qkv[:, 1024:1536], start=True, stop=True).then_inc(s_v, 1)
                    if t := tile(ATT):
                        probs_transposed(t, 0)
                    if t := tile(WO):
                        if t.i == 0:
                            pe.wait_ge(s_wow, t.loads() * 16)
                        pe.wait_ge(s_oT, t.count())
                        if before is not None:
                            pe.wait_ge(s_xn, before * 2 + 2)
                        for c in range(PAIRS):
                            last = mm(OB[:, 0:DIM], oT[:, c, :], w_o[:, c, :], start=(c == 0), stop=(c == PAIRS - 1))
                        last.then_inc(s_y, 1)
                    if t := tile(ATT):
                        b = t.i % 2
                        pe.wait_ge(s_vlo[b], t.count(every=2, unit=16))
                        if t.it is not None or t.c > 0:
                            pe.wait_ge(s_vup[1 - b], t.count(back=1, every=2, unit=16))
                        probs_transposed(t, 1)
                    if t := tile(TH):
                        pe.wait_ge(s_h[t.i % 4], t.count(every=4, unit=32))
                        need(pe, s_vown, t.count(back=1))
                        need(pe, s_hT, t.count(back=1))
                        transpose(VB[:, 0:P], h[:, t.i % 4, :]).then_inc(s_th, 1)
                    if t := tile(FFN_IN):
                        pe.wait_ge(s_h2n, t.count())
                        if t2 := tile(QKV):
                            pe.wait_ge(s_vown, t2.count())
                        else:
                            pe.wait_ge(s_h2T, t.count(back=1))
                        transpose(VB[:, P:2 * P], h2n[:, t.i % 2, :]).then_inc(s_th2, 1)
                    if t := tile(TQK):
                        need(pe, s_p, t.count(back=1, unit=2))
                        masked(t, 0)
                    if t := tile(ATT):
                        b = t.i % 2
                        pe.wait_ge(s_pTv, t.count())
                        pe.wait_ge(s_pTa, t.count())
                        need(pe, s_xm, t.count(back=1))
                        for w, v in ((0, v_prev), (1, v_own)):
                            for hd in range(HEADS):
                                last = mm(OB[64 * w:64 * w + 64, hd * DH:hd * DH + DH],
                                          pT[:, hd, 64 * w:64 * w + 64], v[:, t.i % 4, hd * DH:hd * DH + DH],
                                          start=True, stop=True)
                        last.then_inc(s_o, 1)
                    if t := tile(TQK):
                        b = t.i % 2
                        pe.wait_ge(s_qr, t.count())
                        pe.wait_ge(s_kr, t.count())
                        if t2 := tile(QKV):
                            pe.wait_ge(s_sq, t2.count())
                        for m, src in ((1, k_r), (0, q_r)):
                            for c in range(PAIRS):
                                last = transpose(QK[:, m * 512 + c * P:m * 512 + c * P + P], src[:, b, c * P:c * P + P])
                            last.then_inc(s_tqk, 1)
                    if t := tile(ATT):
                        pe.wait_ge(s_on, t.count())
                        for c in range(PAIRS):
                            last = transpose(OB[:, c * P:c * P + P], o_n[:, c * P:c * P + P])
                        last.then_inc(s_to, 1)
                    if t := tile(TQK):
                        i, b = t.i, t.i % 2
                        masked(t, 1)
                        pe.wait_ge(s_qT, t.count())
                        pe.wait_ge(s_kT, t.count())
                        sc = SC[:, :].rearrange("q (c e b k) -> q c e b k", c=PAIRS, e=2, b=2)
                        for half in range(2):
                            chunks = (2 * half, 2 * half + 1)
                            for c in chunks:
                                last = mm(sc[:, c, :, 0, :], qT[:, b, c, :], kT[:, b, c, :, 0:64],
                                          start=False, stop=True, skip_group_check=True)
                            for c in chunks:
                                if i:
                                    last = mm(sc[0:64, c, :, 1, :], qT[:, b, c, 0:64], kT[:, 1 - b, c, :, 64:128],
                                              start=False, stop=True, skip_group_check=True)
                            for c in chunks:
                                last = mm(sc[64:128, c, :, 1, :], qT[:, b, c, 64:128], kT[:, b, c, :, 64:128],
                                          start=False, stop=True, skip_group_check=True)
                            last.then_inc(s_s, 1)
                    if burst is not None:
                        ffn(tile, burst)
                return f

            def ffn(tile, n):
                last_in = tile(FFN_IN)
                pe.wait_ge(s_h2T, last_in.count())
                pe.wait_ge(s_ffnw, last_in.loads() * 96)

                def w1_pair(k):
                    half, c = divmod(k, 3)
                    at, m = CH[c]
                    a, g = banks(k)
                    if k >= 2:
                        pe.wait_ge(s_act2, n * 6 + (k - 1))
                    rhs = h2T[:, half * 512:half * 512 + 512]
                    mm(g[0:m], w_1[:, HID + at:HID + at + m], rhs, start=True, stop=True)
                    mm(a[0:m], w_1[:, at:at + m], rhs, start=True, stop=True).then_inc(s_w1, 1)

                def w2_half(half):
                    dst = VB if half == 0 else OB
                    pe.wait_ge(s_act2, n * 6 + (3 * half + 3))
                    if half == 0:
                        if t := tile(TH):
                            pe.wait_ge(s_hT, t.count())
                    elif t := tile(ATT):
                        pe.wait_ge(s_oT, t.count())
                    for q in range(HALF):
                        for c, (at, m) in enumerate(CH):
                            last = mm(dst[:, q * DIM:q * DIM + DIM], act2[0:m, half, c, q * P:q * P + P],
                                      w_2[0:m, c, :], start=(c == 0), stop=(c == 2))
                    last.then_inc(s_w2, 1)

                for k in range(6):
                    w1_pair(k)
                w2_half(0)
                w2_half(1)

            pipeline(pe, step(0), 0)
            stack_done(pe, 0)

            with pe.Fori(0, SEQS) as s:
                pe.wait_ge(g_y, s * 2 + (SEQS + 1))
                for i in range(TILES):
                    last = transpose(TT[:, i * P:i * P + P], y_in[:, i, :])
                last.then_inc(g_ty, 1)
                pe.wait_ge(g_yT, s + 1)
                for i in range(TILES):
                    if i >= 2:
                        pe.wait_ge(g_z, s * TILES + (i - 1))
                    mm(QK[:, i % 2 * 512:i % 2 * 512 + 384], h2T[:, i * P:i * P + P],
                       w_kqv[:, :, :].rearrange("p a b -> p (a b)"), start=True, stop=True).then_inc(g_pr, 1)
                zn = act2[:].rearrange("p a b c -> p (a b c)").rearrange("p (i m) -> p i m", i=TILES)
                for m, dst in ((0, TT), (1, SC)):
                    pe.wait_ge(g_zn, s * 3 + (m + 1))
                    for i in range(TILES):
                        last = transpose(dst[:, i * P:i * P + P], zn[:, i, m * DIM:m * DIM + DIM])
                    last.then_inc(g_tk, 1)
                pe.wait_ge(g_kT, s * 2 + 2)
                for i in range(TILES + 2):
                    if i < TILES:
                        dst = QK if i % 2 else SC
                        if i >= 2:
                            pe.wait_ge(g_p, s * TILES + (i - 1))
                        for m in range(2):
                            last = mm(dst[:, m * 512:m * 512 + 512], rope_c[:, i * P:i * P + P],
                                      rope_s[:, m * 512:m * 512 + 512], start=True, stop=True)
                        last.then_inc(g_s, 1)
                    if 0 <= (k := i - 1) < TILES:
                        pe.wait_ge(g_p, s * TILES + (k + 1))
                        if k:
                            pe.wait_ge(g_pTv, s * TILES + k)
                            pe.wait_ge(g_pTa, s * TILES + k)
                        for m in range(TILES):
                            last = transpose(TT[:, m * P:m * P + P], probs[:, k % 2, m, :])
                        last.then_inc(g_tp, 1)
                    if 0 <= (k := i - 2):
                        pe.wait_ge(g_pTv, s * TILES + (k + 1))
                        pe.wait_ge(g_pTa, s * TILES + (k + 1))
                        if k >= 2:
                            pe.wait_ge(g_x2, s * TILES + (k - 1))
                        if k == 0:
                            pe.wait_ge(g_vg, s * 2 + 2)
                        dst = OB if k % 2 else VB
                        src = pT2 if k % 2 else pT
                        for m in range(TILES):
                            last = mm(dst[:, 0:DIM], src[:, m, :], v_g[:, m, :], start=(m == 0), stop=(m == TILES - 1))
                        last.then_inc(g_o, 1)
                pe.wait_ge(g_x2, s * TILES + TILES)

            pipeline(pe, step(1), 1)

        @block.vector
        def _(dve):
            v = nc.vector
            v.memset(zeros[:], 0.0).then_inc(s_zero, 1)
            v.memset(v_prev[:], 0.0).then_inc(s_zero, 1)
            v.memset(kT[:], 0.0).then_inc(s_zero, 1)
            v.memset(b_1all[:], 0.0).then_inc(s_zero, 1)
            v.memset(mhalf[:], -0.5).then_inc(s_zero, 1)
            v.memset(epsilon[:], EPS).then_inc(s_zero, 1)
            def stats(tile, slot):
                return v.bn_stats(st_g[:, slot, :], tile)

            def stats_fence(n):
                dve.wait_ge(g_st, n * 2 - 1)
                v.tensor_copy(fence[:], zeros[:, 0:1]).then_inc(g_st, 1)

            def aggregate(n, slot):
                for k in range(slot, slot + n):
                    last = v.bn_aggr(mv_g[:, k, :], st_g[:, k, :])
                last.then_inc(g_mv, 1)

            def normalise(dst, src, slot):
                for k in range(TILES):
                    m = slot + k
                    last = v.tensor_scalar(dst[:, k, :], src[:, k, :], mv_g[:, m, 0:1], rs_g[:, m:m + 1],
                                           ALU.subtract, ALU.mult)
                return last

            dve.wait_ge(s_zero, ZEROED)
            for s in range(SEQS):
                dve.wait_ge(g_in[s], 16)
                for k in range(TILES):
                    last = stats(arrived[s][:, k, :], s * TILES + k)
                last.then_inc(g_st, 1)
                stats_fence(s + 1)
                aggregate(TILES, s * TILES)
            for s in range(SEQS):
                dve.wait_ge(g_rs, s + 1)
                normalise(arrived[s], arrived[s], s * TILES).then_inc(g_y, 1)
            dve.wait_ge(s_w, N_CONST)
            v.tensor_copy(ident_b[:], ident[:]).then_inc(s_cast, 1)
            v.tensor_copy(mask_b[:], mask_f[:]).then_inc(s_cast, 1)
            for l in range(DEPTH):
                v.tensor_tensor(rope_all[:, l].rearrange("p t a b d -> p t (a b d)"),
                                rope_all[:, l].rearrange("p t a b d -> p t (a b d)"),
                                gains[:, l].rearrange("p a b d -> p (a b d)").unsqueeze(1).to_broadcast([P, TILES, 4 * DH]),
                                ALU.mult).then_inc(s_fold, 1)
            dve.wait_ge(s_b1mm, 1)
            dve.wait_ge(s_zero, ZEROED)
            for l in range(DEPTH):
                for c in range(6):
                    n = CH[c % 3][1]
                    k = l * 6 + c
                    last = v.tensor_tensor(b_1all[0:n, l, c:c + 1], VB[0:n, k:k + 1], b_1raw[0:n, l, c:c + 1], ALU.add)
            last.then_inc(s_b1, 1)

            def aggregate2(t):
                v.bn_aggr(mv2[:, t.i % 2, :], st2[:, t.i % 2, :]).then_inc(s_mv2, 1)

            def step(tile, burst, before):
                if t := tile(ATT):
                    b = t.i % 2
                    need(dve, s_p, t.count(back=2, unit=2))
                    dve.wait_ge(s_qg, t.count())
                    for half in range(2):
                        hd = slice(4 * half, 4 * half + 4)
                        dve.wait_ge(s_s, t.count(unit=2) + (half - 1))
                        v.tensor_reduce(top[:, b, hd], SC[:, half * 512:half * 512 + 512].rearrange(
                            "q (h k) -> q h k", h=4), AX, ALU.max).then_inc(s_mx, 1)
                        dve.wait_ge(s_mx, t.count(unit=2) + (half - 1))
                        if half == 0 and (t2 := tile(FFN_IN)):
                            dve.wait_ge(s_st2, t2.count())
                        v.scalar_tensor_tensor(out=shift[:, b, hd], in0=top[:, b, hd], scalar=-1.0, in1=qgain[:, b, hd],
                                               op0=ALU.mult, op1=ALU.mult).then_inc(s_sh, 1)
                if t := tile(FFN_IN):
                    if not tile(ATT):
                        dve.wait_ge(s_st2, t.count())
                    aggregate2(t)
                if before is not None:
                    for half in range(2):
                        dve.wait_ge(s_w2, before * 2 + (half + 1))
                        if half == 0:
                            dve.wait_ge(s_xb2, tile(FFN_IN + 1).count())
                            dve.wait_ge(s_st, before * 32 + 16)
                        src = (VB if half == 0 else OB)[:, :].rearrange("p (t c) -> p t c", t=HALF)
                        v.tensor_tensor(x_new[:, half * HALF:half * HALF + HALF, :], src,
                                        x_b2[:, half * HALF:half * HALF + HALF, :], ALU.add).then_inc(s_xn, 1)
                if t := tile(QKV):
                    i = t.i
                    dve.wait_ge(s_rope[i], t.loads() * 16)
                    need(dve, s_qr, t.count(back=1))
                    need(dve, s_ka, t.count(back=1))
                    for m, signal in ((0, s_q), (1, s_k)):
                        dve.wait_ge(signal, t.count())
                        src = qk(QK[:, :])[:, m]
                        v.tensor_tensor(qk(rope_c[:])[:, m], src,
                                        rope[:, i, m, 0:1, :].to_broadcast([P, HEADS, DH]), ALU.mult)
                        sin = rope[:, i, m, 1:2, :]
                        for half in range(2):
                            a, o = 32 * half, 32 * (1 - half)
                            last = v.tensor_tensor(qk(rope_s[:])[:, m, :, a:a + 32], src[:, :, o:o + 32],
                                                   sin[:, :, a:a + 32].to_broadcast([P, HEADS, 32]), ALU.mult)
                    last.then_inc(s_rot, 1)
                if t := tile(FFN_IN):
                    b, k = t.i % 2, t.i % 4
                    dve.wait_ge(s_rs2, t.count())
                    need(dve, s_th2, t.count(back=2))
                    v.tensor_scalar(h2n[:, b, :], h2[:, k, :], mv2[:, b, 0:1], rstd2[:, b, :],
                                    ALU.subtract, ALU.mult).then_inc(s_h2n, 1)
                if t := tile(WO):
                    i, b = t.i, t.i % 2
                    dve.wait_ge(s_y, t.count())
                    dve.wait_ge(s_x[i], t.count(every=TILES, unit=16))
                    need(dve, s_xb2, t.count(back=2))
                    v.tensor_tensor(x_mid[:, i, :], OB[:, 0:DIM], x_att[:, i, :], ALU.add).then_inc(s_xm, 1)
                if t := tile(ATT):
                    dve.wait_ge(s_tp, t.count(unit=2) - 1)
                    need(dve, s_o, t.count(back=1))
                    v.tensor_copy(pT[:, 0:4, :], TT[:, 0:512].rearrange("k (h q) -> k h q", h=4)).then_inc(s_pTv, 1)
                if t := tile(ATT):
                    b = t.i % 2
                    dve.wait_ge(s_p, t.count(unit=2))
                    v.reciprocal(rsums[:, b, :], psums[:, b, :]).then_inc(s_rsum, 1)
                    dve.wait_ge(s_rsum, t.count())
                    dve.wait_ge(s_o, t.count())
                    need(dve, s_to, t.count(back=1))
                    v.tensor_tensor(o_n[:].rearrange("q (h d) -> q h d", h=HEADS),
                                    OB[:, :].rearrange("q (h d) -> q h d", h=HEADS),
                                    rsums[:, b, :].unsqueeze(2).to_broadcast([P, HEADS, DH]), ALU.mult).then_inc(s_on, 1)
                if t := tile(TQK):
                    dve.wait_ge(s_tqk, t.count(unit=2))
                    need(dve, s_s, t.count(back=1, unit=2))
                    v.tensor_copy(qT[:, t.i % 2], QK[:, 0:512].rearrange("d (c t) -> d c t", c=PAIRS)).then_inc(s_qT, 1)
                if t := tile(QKV):
                    b = t.i % 2
                    dve.wait_ge(s_sq, t.count())
                    need(dve, s_rn, t.count(back=2))
                    v.tensor_reduce(norm2[:, b, :], sq[:].rearrange("p (h d) -> p h d", d=DH), AX, ALU.add).then_inc(s_n2, 1)
                    dve.wait_ge(s_n2, t.count())
                    v.tensor_scalar(clip2[:, b, 8:16], norm2[:, b, 8:16], 1e-24, None, ALU.max).then_inc(s_cl, 1)
                    need(dve, s_qg, t.count(back=2))
                    v.tensor_scalar(clip2[:, b, 0:8], norm2[:, b, 0:8], 1e-24, QK_SCALE ** -2,
                                    ALU.max, ALU.mult).then_inc(s_cl, 1)
                if t := tile(WO):
                    b, k = t.i % 2, t.i % 4
                    dve.wait_ge(s_h2[k], t.count(every=4, unit=48))
                    v.bn_stats(st2[:, b, :], h2[:, k, :]).then_inc(s_st2, 1)
                if burst is not None:
                    n = burst
                    for k in range(6):
                        half, c = divmod(k, 3)
                        m = CH[c][1]
                        dve.wait_ge(s_gelu, n * 6 + (k + 1))
                        v.scalar_tensor_tensor(out=act2[0:m, half, c, :], in0=banks(k)[0][0:m], scalar=b_1[0:m, c:c + 1],
                                               in1=gelu[0:m, k % 2, :], op0=ALU.add, op1=ALU.mult).then_inc(s_act2, 1)

            pipeline(dve, step, 0)
            stack_done(dve, 0)

            with dve.Fori(0, SEQS) as s:
                lot, rs = s * 3 + SEQS, s * 5 + SEQS
                dve.wait_ge(g_ld, s * 32 + 32)
                v.scalar_tensor_tensor(out=flat(x_mid), in0=flat(x_b2), scalar=0.5, in1=flat(x_att),
                                       op0=ALU.mult, op1=ALU.add).then_inc(g_x1, 1)
                dve.wait_ge(g_x1, s + 1)
                for k in range(TILES):
                    last = stats(x_mid[:, k, :], LN_IN + k)
                last.then_inc(g_st, 1)
                stats_fence(lot + 1)
                aggregate(TILES, LN_IN)
                dve.wait_ge(g_rs, rs + 1)
                normalise(y_in, x_mid, LN_IN).then_inc(g_y, 1)
                z = act2[:].rearrange("p a b c -> p (a b c)").rearrange("p (i m) -> p i m", i=TILES)
                for i in range(TILES + 1):
                    if i < TILES:
                        dve.wait_ge(g_pr, s * TILES + (i + 1))
                        v.tensor_tensor(z[:, i, :], QK[:, i % 2 * 512:i % 2 * 512 + 384], b_kqv[:], ALU.add).then_inc(g_z, 1)
                    if i:
                        dve.wait_ge(g_z, s * TILES + i)
                        for m in range(3):
                            last = stats(z[:, i - 1, m * DIM:m * DIM + DIM], KQV + m * TILES + i - 1)
                last.then_inc(g_st, 1)
                stats_fence(lot + 2)
                aggregate(3 * TILES, KQV)
                for m in range(3):
                    dve.wait_ge(g_rs, rs + (m + 2))
                    zz = z[:, :, m * DIM:m * DIM + DIM]
                    normalise(zz, zz, KQV + m * TILES).then_inc(g_zn, 1)
                dve.wait_ge(g_sto, (s * 2 + SEQS) * 16)
                for i in range(TILES + 2):
                    if i < TILES:
                        b = i % 2
                        dve.wait_ge(g_s, s * TILES + (i + 1))
                        v.tensor_reduce(mx_g[:, b:b + 1], (QK if b else SC)[:, :], AX, ALU.max).then_inc(g_mx, 1)
                        dve.wait_ge(g_mx, s * TILES + (i + 1))
                        v.tensor_scalar(nm_g[:, b:b + 1], mx_g[:, b:b + 1], -1.0, None, ALU.mult).then_inc(g_nm, 1)
                    if 0 <= (k := i - 1) < TILES:
                        b = k % 2
                        dve.wait_ge(g_tp, s * TILES + (k + 1))
                        if k >= 2:
                            dve.wait_ge(g_o, s * TILES + (k - 1))
                        v.tensor_copy((pT2 if b else pT)[:, 0:4, :],
                                      TT[:, 0:512].rearrange("k (h q) -> k h q", h=4)).then_inc(g_pTv, 1)
                        if k >= 2:
                            dve.wait_ge(g_x2, s * TILES + (k - 1))
                        v.reciprocal(rl_g[:, b:b + 1], sm_g[:, b:b + 1]).then_inc(g_rl, 1)
                    if 0 <= (k := i - 2):
                        b = k % 2
                        dve.wait_ge(g_rl, s * TILES + (k + 1))
                        dve.wait_ge(g_o, s * TILES + (k + 1))
                        if k == 0:
                            dve.wait_ge(g_xy, s + 1)
                        v.scalar_tensor_tensor(out=x_2[:, k, :], in0=(OB if b else VB)[:, 0:DIM], scalar=rl_g[:, b:b + 1],
                                               in1=sq[:, k * DIM:k * DIM + DIM], op0=ALU.mult, op1=ALU.add).then_inc(g_x2, 1)
                        if k:
                            dve.wait_ge(g_x2, s * TILES + k)
                            stats(x_2[:, k - 1, :], LN_OUT + k - 1)
                dve.wait_ge(g_x2, s * TILES + TILES)
                stats(x_2[:, TILES - 1, :], LN_OUT + TILES - 1).then_inc(g_st, 1)
                stats_fence(lot + 3)
                aggregate(TILES, LN_OUT)
                dve.wait_ge(g_rs, rs + 5)
                normalise(x_new, x_2, LN_OUT).then_inc(g_y, 1)

            pipeline(dve, step, 1)
            for s in range(SEQS):
                dve.wait_ge(g_fin[s], 32)
                v.scalar_tensor_tensor(out=flat(kept[s]), in0=flat(half_step[s]), scalar=0.5, in1=flat(kept[s]),
                                       op0=ALU.mult, op1=ALU.add).then_inc(g_x2, 1)

        @block.scalar
        def _(act):
            def copy(dst, src):
                return nc.scalar.activation(dst, src, ACT.Copy)

            def step(tile, burst, before):
                if t := tile(ATT):
                    b = t.i % 2
                    need(act, s_tp, t.count(back=2, unit=2))
                    need(act, s_rsum, t.count(back=2))
                    for half in range(2):
                        act.wait_ge(s_sh, t.count(unit=2) + (half - 1))
                        for hd in range(4 * half, 4 * half + 4):
                            last = nc.scalar.activation(probs[:, b, hd, :], SC[:, hd * P:hd * P + P], ACT.Exp,
                                                        bias=shift[:, b, hd:hd + 1], scale=qgain[:, b, hd:hd + 1],
                                                        accum_out=psums[:, b, hd:hd + 1])
                        last.then_inc(s_p, 1)
                if t := tile(QKV):
                    b = t.i % 2
                    act.wait_ge(s_v, t.count())
                    need(act, s_o, t.count(back=3))
                    if t.it is not None or t.c >= 2:
                        act.wait_ge(s_vlo[b], t.count(back=2, every=2, unit=16))
                        act.wait_ge(s_vup[b], t.count(back=2, every=2, unit=16))
                    copy(v_own[:, t.i % 4, :], VB[:]).then_inc(s_vown, 1)
                if t := tile(ATT):
                    act.wait_ge(s_tp, t.count(unit=2))
                    need(act, s_o, t.count(back=1))
                    copy(pT[:, 4:8, :], TT[:, 512:1024].rearrange("k (h q) -> k h q", h=4)).then_inc(s_pTa, 1)
                if t := tile(QKV):
                    need(act, s_n2, t.count(back=1))
                    act.wait_ge(s_rot, t.count())
                    nc.scalar.activation(sq[:], QK[:], ACT.Square).then_inc(s_sq, 1)
                if t := tile(TH):
                    act.wait_ge(s_th, t.count())
                    if t2 := tile(FFN_IN):
                        act.wait_ge(s_th2, t2.count())
                    need(act, s_v, t.count(back=2))
                    copy(hT[:, t.i % 2, :], VB[:, 0:P]).then_inc(s_hT, 1)
                if t := tile(FFN_IN):
                    act.wait_ge(s_th2, t.count())
                    copy(h2T[:, t.i * P:t.i * P + P], VB[:, P:2 * P]).then_inc(s_h2T, 1)
                if t := tile(TQK):
                    b = t.i % 2
                    act.wait_ge(s_tqk, t.count(unit=2) - 1)
                    need(act, s_s, t.count(back=1, unit=2))
                    for e in range(2):
                        last = copy(kT[64 * e:64 * e + 64, b, :, e, :],
                                    QK[64 * e:64 * e + 64, 512:1024].rearrange("d (c t) -> d c t", c=PAIRS))
                    last.then_inc(s_kT, 1)
                if t := tile(ATT):
                    act.wait_ge(s_to, t.count())
                    need(act, s_y, t.count(back=1))
                    copy(oT[:], OB[:].rearrange("d (c t) -> d c t", c=PAIRS)).then_inc(s_oT, 1)
                if burst is not None:
                    n = burst
                    for k in range(6):
                        c = k % 3
                        m = CH[c][1]
                        act.wait_ge(s_w1, n * 6 + (k + 1))
                        if k >= 2:
                            act.wait_ge(s_act2, n * 6 + (k - 1))
                        nc.scalar.activation(gelu[0:m, k % 2, :], banks(k)[1][0:m], ACT.Gelu,
                                             bias=b_1[0:m, 3 + c:4 + c]).then_inc(s_gelu, 1)

            act.wait_ge(s_zero, ZEROED)
            pipeline(act, step, 0)
            stack_done(act, 0)

            with act.Fori(0, SEQS) as s:
                act.wait_ge(g_ty, s + 1)
                copy(h2T[:], TT[:]).then_inc(g_yT, 1)
                for m, src, dst in ((0, TT, rope_c), (1, SC, rope_s)):
                    act.wait_ge(g_tk, s * 2 + (m + 1))
                    nc.scalar.activation(dst[:], src[:], ACT.Identity, bias=kq_gb[:, 2 * m + 1:2 * m + 2],
                                         scale=kq_gb[:, 2 * m:2 * m + 1]).then_inc(g_kT, 1)
                for i in range(TILES + 1):
                    if i < TILES:
                        b = i % 2
                        act.wait_ge(g_nm, s * TILES + (i + 1))
                        if i >= 2:
                            act.wait_ge(g_tp, s * TILES + (i - 1))
                            act.wait_ge(g_rl, s * TILES + (i - 1))
                        nc.scalar.activation(probs[:, b].rearrange("p a b -> p (a b)"), (QK if b else SC)[:], ACT.Exp,
                                             bias=nm_g[:, b:b + 1], accum_out=sm_g[:, b:b + 1]).then_inc(g_p, 1)
                    if i:
                        k = i - 1
                        b = k % 2
                        act.wait_ge(g_tp, s * TILES + (k + 1))
                        if k >= 2:
                            act.wait_ge(g_o, s * TILES + (k - 1))
                        copy((pT2 if b else pT)[:, 4:8, :],
                             TT[:, 512:1024].rearrange("k (h q) -> k h q", h=4)).then_inc(g_pTa, 1)

            pipeline(act, step, 1)

        @block.gpsimd
        def _(pool):
            g = nc.gpsimd
            pool.wait_ge(s_zero, ZEROED)

            def rstd(slot, n, lot, parts=1):
                pool.wait_ge(g_mv, lot)
                g.tensor_tensor(ve_g[:, slot:slot + n], mv_g[:, slot:slot + n, 1], epsilon[:, 0:n], ALU.add).then_inc(g_ve, 1)
                pool.wait_ge(g_ve, lot)
                for k in range(slot, slot + n, n // parts):
                    g.tensor_tensor(rs_g[:, k:k + n // parts], ve_g[:, k:k + n // parts], mhalf[:, 0:n // parts],
                                    ALU.pow).then_inc(g_rs, 1)

            for s in range(SEQS):
                rstd(s * TILES, TILES, s + 1)
            pool.wait_ge(s_w, N_CONST)
            for l in range(DEPTH):
                last = g.tensor_scalar(w_1all[:, l, :], w_1raw[:, l, :], ln_gb_sb[:, 0, l:l + 1], None, ALU.mult)
            last.then_inc(s_fold, 1)

            def step(tile, burst, before):
                if t := tile(FFN_IN):
                    i, b = t.i, t.i % 2
                    need(pool, s_mv2, t.count())
                    g.tensor_tensor(ve2[:, b, :], mv2[:, b, 1:2], epsilon[:, 0:1], ALU.add).then_inc(s_ve2, 1)
                    pool.wait_ge(s_ve2, t.count())
                    g.tensor_tensor(rstd2[:, b, :], ve2[:, b, :], mhalf[:, 0:1], ALU.pow).then_inc(s_rs2, 1)
                    if i == 0:
                        pool.wait_ge(s_ffnw, t.loads() * 96)
                        k = t.count(back=TILES, every=TILES, unit=2)
                        need(pool, s_xn, k)
                    pool.wait_ge(s_xm, t.count())
                    g.tensor_tensor(x_b2[:, i, :], x_mid[:, i, :], b_2[:], ALU.add).then_inc(s_xb2, 1)
                if t := tile(QKV + 1):
                    b = t.i % 2
                    pool.wait_ge(s_cl, t.count(unit=2))
                    need(pool, s_p, t.count(back=2, unit=2))
                    g.tensor_tensor(qgain[:, b, :], clip2[:, b, 0:8], mhalf[:, 0:8], ALU.pow).then_inc(s_qg, 1)
                if t := tile(QKV):
                    b = t.i % 2
                    pool.wait_ge(s_rot, t.count())
                    need(pool, s_tqk, t.count(back=2, unit=2))
                    g.tensor_tensor(q_r[:, b, :], rope_c[:, 0:512], rope_s[:, 0:512], ALU.add).then_inc(s_qr, 1)
                    need(pool, s_kr, t.count(back=1))
                    g.tensor_tensor(k_a[:], rope_c[:, 512:1024], rope_s[:, 512:1024], ALU.add).then_inc(s_ka, 1)
                    pool.wait_ge(s_cl, t.count(unit=2) - 1)
                    g.tensor_tensor(rnorm[:, b, :], clip2[:, b, 8:16], mhalf[:, 0:8], ALU.pow).then_inc(s_rn, 1)
                    pool.wait_ge(s_rn, t.count())
                    pool.wait_ge(s_ka, t.count())
                    g.tensor_tensor(k_r[:, b, :].rearrange("p (h d) -> p h d", h=HEADS),
                                    k_a[:].rearrange("p (h d) -> p h d", h=HEADS),
                                    rnorm[:, b, :].unsqueeze(2).to_broadcast([P, HEADS, DH]), ALU.mult).then_inc(s_kr, 1)

            pipeline(pool, step, 0)
            stack_done(pool, 0)

            with pool.Fori(0, SEQS) as s:
                rstd(LN_IN, TILES, s * 3 + (SEQS + 1))
                pool.wait_ge(g_y, s * 2 + (SEQS + 1))
                g.tensor_tensor(sq[:], flat(x_mid), gelu[:].rearrange("p a b -> p (a b)"), ALU.add).then_inc(g_xy, 1)
                rstd(KQV, 3 * TILES, s * 3 + (SEQS + 2), parts=3)
                pool.wait_ge(g_zn, s * 3 + 3)
                z = act2[:].rearrange("p a b c -> p (a b c)").rearrange("p (i m) -> p i m", i=TILES)
                vz = z[:, :, 2 * DIM:3 * DIM]
                scaled = k_r[:].rearrange("p a (t c) -> p (a t) c", c=DIM)
                g.tensor_tensor(scaled, vz, v_gb[:, 0:1, :].to_broadcast([P, TILES, DIM]), ALU.mult).then_inc(g_vg, 1)
                pool.wait_ge(g_vg, s * 2 + 1)
                g.tensor_tensor(v_g[:], scaled, v_gb[:, 1:2, :].to_broadcast([P, TILES, DIM]), ALU.add).then_inc(g_vg, 1)
                rstd(LN_OUT, TILES, s * 3 + (SEQS + 3))

            pipeline(pool, step, 1)


ZEROED = 6
N_CONST = 15 * 16


def tables():
    f = np.float32
    half_idx = np.arange(0, DH, 2, dtype=f)
    inv_freq = (f(1.0) / np.power(f(10000.0), half_idx / f(DH))).astype(f)
    t = np.arange(SLEN, dtype=f)
    ang = (t[:, None] * inv_freq[None, :]).astype(f)
    base = ((half_idx + f(0.4 * DH)) / f(1.4 * DH)).astype(f)
    power = ((t - f(SLEN // 2)) / f(WIN // 2)).astype(f)
    scale = np.power(base[None, :], power[:, None]).astype(f)
    cos, sin = np.cos(ang), np.sin(ang)
    rope = np.zeros((SLEN, 2, 2, DH), f)
    for m, sc in ((0, scale), (1, f(1.0) / scale)):
        rope[:, m, 0, :32] = rope[:, m, 0, 32:] = cos * sc
        rope[:, m, 1, :32] = -sin * sc
        rope[:, m, 1, 32:] = sin * sc
    rope = rope.reshape(TILES, P, 2, 2, DH).transpose(1, 0, 2, 3, 4)
    r = np.arange(WIN)[:, None]
    c = np.arange(WIN)[None, :]
    own, prev = (c <= r), (c >= r)
    allowed = np.zeros((2, P, P), bool)
    allowed[:, :64, :64] = own
    allowed[:, 64:, :64] = prev
    allowed[0, :64, 64:] = prev
    allowed[:, 64:, 64:] = own
    mask = np.where(allowed, 0.0, -1e30).astype(f).transpose(1, 0, 2)
    return (np.ascontiguousarray(rope), np.ascontiguousarray(mask), np.eye(P, dtype=f))


def kernel(**inputs):
    import concourse.bacc as bacc
    from concourse.bass_utils import run_bass_kernel_spmd

    a = {k: np.asarray(v) for k, v in inputs.items()}
    A, L = "L0_attn_", "L0_ffn_"
    rope, mask, ident = tables()
    b1 = np.zeros((DEPTH, 2, 3 * P), a[L + "b1"].dtype)
    b1[:, :, :HID] = a[L + "b1"].reshape(DEPTH, 2, HID)
    b1 = b1.reshape(DEPTH, 6, P).transpose(2, 0, 1)
    arrays = {
        "x_in": a[A + "input_sequence"],
        "w_attn": np.stack([a[A + "Wk"], a[A + "Wq"], a[A + "Wv"]], axis=1),
        "b_attn": np.concatenate([a[A + "bk"], a[A + "bq"], a[A + "bv"]]),
        "kq_gain": np.stack([a[A + "gk"], a[A + "betak"], a[A + "gq"], a[A + "betaq"]], axis=1),
        "v_gain": np.stack([a[A + "gv"], a[A + "betav"]]),
        "wqkv": a[L + "wqkv"],
        "qk_gain": np.stack([a[L + "q_scale"], a[L + "k_scale"]], axis=1),
        "wo_in": a[L + "wo"],
        "ln_gb": np.stack([a[L + "ln_g"].T, a[L + "ln_b"].T], axis=1),
        "w1_in": a[L + "w1"], "b1_in": b1, "w2_in": a[L + "w2"], "b2_in": a[L + "b2"],
        "rope_in": rope, "mask_in": mask, "ident_in": ident,
    }
    arrays = {k: np.ascontiguousarray(v) for k, v in arrays.items()}
    nc = bacc.Bacc("TRN2", target_bir_lowering=False, num_devices=1)
    args = [nc.dram_tensor(k, v.shape, mybir.dt.from_np(v.dtype), kind="ExternalInput").ap() for k, v in arrays.items()]
    out = nc.dram_tensor("out", [SEQS, SLEN, DIM], F32, kind="ExternalOutput").ap()
    build(nc, *args, out)
    r = run_bass_kernel_spmd(nc, [arrays], core_ids=[0])
    return r.results[0]["out"]
```

```python
from contextlib import ExitStack

import numpy as np
import concourse.bass as bass
from concourse import mybir

ALU = mybir.AluOpType
ACT = mybir.ActivationFunctionType
AX = mybir.AxisListType.X
F32 = mybir.dt.float32
BF16 = mybir.dt.bfloat16
F32R = mybir.dt.float32r

P = 128
DIM = 128
HEADS = 8
DH = 64
WIN = 64
INNER = HEADS * DH
HID = DIM * 4 * 2 // 3
DEPTH = 2
SEQS = 4
SLEN = 1024
TILES = SLEN // P
ITERS = DEPTH * SEQS
NT = ITERS * TILES
PAIRS = HEADS // 2
CH = [(0, 128), (128, 128), (256, HID - 256)]
EPS = 1e-5
QK_SCALE = float(DH) ** 0.5
HALF = TILES // 2

TH, QKV, TQK, ATT, WO, FFN_IN = 1, 2, 4, 5, 6, 7
BURST = TILES + FFN_IN - 1
LAST = (ITERS - 1) * TILES + BURST

KQV, LN_OUT, LN_IN = 0, 3 * TILES, 4 * TILES
SLOTS = 5 * TILES


class Tile:

    def __init__(self, it, c, stack):
        self.it, self.c = it, c
        self.i = c % TILES
        self.first = stack * NT

    def count(self, back=0, every=1, unit=1):
        c = self.c - back + self.first
        k = (c // every + 1) * unit
        return k if self.it is None else self.it * (TILES // every * unit) + k

    def loads(self):
        k = self.c // TILES
        layer = (k if self.it is None else self.it + k) // SEQS
        return layer + (self.first // NT * DEPTH + 1)


def need(eng, sem, count):
    if not isinstance(count, int) or count > 0:
        eng.wait_ge(sem, count)


def pipeline(eng, step, stack):

    def tile_of(it, g):
        def f(skew):
            c = g - skew
            if it is None and not 0 <= c < NT:
                return None
            return Tile(it, c, stack)
        return f

    def burst_of(it, g):
        if (g - BURST) % TILES or (it is None and g < BURST):
            return None
        n = (g - BURST) // TILES + stack * ITERS
        return n if it is None else it + n

    for g in range(TILES):
        step(tile_of(None, g), burst_of(None, g), None)
    with eng.Fori(1, ITERS) as it:
        for j in range(TILES):
            step(tile_of(it, j), burst_of(it, j), burst_of(it, j - 1))
    for g in range(NT, LAST + 2):
        step(tile_of(None, g), burst_of(None, g), burst_of(None, g - 1))


def build(nc, x_in, w_attn, b_attn, kq_gain, v_gain, wqkv, qk_gain, wo_in, ln_gb, w1_in, b1_in, w2_in,
          b2_in, rope_in, mask_in, ident_in, out):
    stream = nc.dram_tensor("stream", [DEPTH + 1, SEQS, SLEN + 1, DIM], F32, kind="Internal").ap()
    rope_d = nc.dram_tensor("rope_d", [DEPTH, P, TILES, 2, 2, DH], F32, kind="Internal").ap()
    qkv_d = nc.dram_tensor("qkv_d", [DEPTH, P, 2, 3 * INNER], F32, kind="Internal").ap()
    w1_d = nc.dram_tensor("w1_d", [DEPTH, P, 2, 2 * HID], F32, kind="Internal").ap()
    mid = nc.dram_tensor("mid", [SEQS, SLEN, DIM], F32, kind="Internal").ap()

    with ExitStack() as ctx:
        def sb(name, shape, dt=F32):
            return ctx.enter_context(nc.sbuf_tensor(name, shape, dt))

        def ps(name, cols):
            return ctx.enter_context(nc.psum_tensor(name, [P, cols], F32))

        def sem(name):
            return ctx.enter_context(nc.semaphore(name))

        def sems(name, n):
            return [sem(f"{name}{k}") for k in range(n)]

        ident = sb("ident", [P, P])
        ident_b = sb("ident_b", [P, P], BF16)
        mask_f = sb("mask_f", [P, 2, P])
        mask_b = sb("mask_b", [P, 2, P], BF16)
        zeros = sb("zeros", [P, DIM])
        mhalf = sb("mhalf", [P, HEADS])
        epsilon = sb("epsilon", [P, HEADS])
        w_qkv = sb("w_qkv", [P, 2, 3 * INNER])
        w_o = sb("w_o", [P, PAIRS, DIM])
        w_1 = sb("w_1", [P, 2, 2 * HID])
        w_2 = sb("w_2", [P, 3, DIM])
        ln_gb_sb = sb("ln_gb_sb", [P, 2, DEPTH])
        b_1raw = sb("b_1raw", [P, DEPTH, 6])
        b_1all = sb("b_1all", [P, DEPTH, 6])
        b_1 = sb("b_1", [P, 6])
        b_2all = sb("b_2all", [P, DEPTH, DIM])
        b_2 = sb("b_2", [P, DIM])
        gains = sb("gains", [P, DEPTH, 2, 2, DH])
        rope = sb("rope", [P, TILES, 2, 2, DH])
        w_kqv = sb("w_kqv", [P, 3, DIM])
        b_kqv = sb("b_kqv", [P, 3 * DIM])
        kq_gb = sb("kq_gb", [P, 4])
        v_gb = sb("v_gb", [P, 2, DIM])

        x_att = sb("x_att", [P, TILES, DIM])
        x_mid = sb("x_mid", [P, TILES, DIM])
        x_b2 = sb("x_b2", [P, TILES, DIM])
        x_new = sb("x_new", [P, TILES, DIM])
        h = sb("h", [P, 4, DIM])
        hT = sb("hT", [P, 2, 2, P])
        sq = sb("sq", [P, 2 * INNER])
        norm2 = sb("norm2", [P, 2, 2 * HEADS])
        clip2 = sb("clip2", [P, 2, 2 * HEADS])
        rnorm = sb("rnorm", [P, 2, HEADS])
        qgain = sb("qgain", [P, 2, HEADS])
        rope_c = sb("rope_c", [P, 2 * INNER])
        rope_s = sb("rope_s", [P, 2 * INNER])
        q_r = sb("q_r", [P, 2, INNER])
        k_a = sb("k_a", [P, INNER])
        k_r = sb("k_r", [P, 2, INNER])
        qT = sb("qT", [P, 2, PAIRS, P])
        kT = sb("kT", [P, 2, PAIRS, 2, P])
        v_own = sb("v_own", [P, TILES, INNER])
        v_prev = sb("v_prev", [P, TILES, INNER])
        top = sb("top", [P, 2, HEADS])
        shift = sb("shift", [P, 2, HEADS])
        probs = sb("probs", [P, 2, HEADS, P])
        psums = sb("psums", [P, 2, HEADS])
        rsums = sb("rsums", [P, 2, HEADS])
        pT = sb("pT", [P, HEADS, P])
        o_n = sb("o_n", [P, INNER])
        oT = sb("oT", [P, PAIRS, P])
        h2 = sb("h2", [P, 4, DIM])
        st2 = sb("st2", [P, 2, 6])
        mv2 = sb("mv2", [P, 2, 2])
        ve2 = sb("ve2", [P, 2, 1])
        rstd2 = sb("rstd2", [P, 2, 1])
        h2n = sb("h2n", [P, 2, DIM])
        h2T = sb("h2T", [P, 2, SLEN])
        gelu = sb("gelu", [P, 2, HALF * P])
        act2 = sb("act2", [P, 2, 3, HALF * P])
        v_g = sb("v_g", [P, TILES, DIM])
        x_2 = sb("x_2", [P, TILES, DIM])
        pT2 = sb("pT2", [P, TILES, P])
        st_g = sb("st_g", [P, SLOTS, 6])
        mv_g = sb("mv_g", [P, SLOTS, 2])
        ve_g = sb("ve_g", [P, SLOTS])
        rs_g = sb("rs_g", [P, SLOTS])
        fence = sb("fence", [P, 1])
        mx_g = sb("mx_g", [P, 2])
        nm_g = sb("nm_g", [P, 2])
        sm_g = sb("sm_g", [P, 2])
        rl_g = sb("rl_g", [P, 2])

        QK = ps("QK", 1024)
        VB = ps("VB", 512)
        SC = ps("SC", 1024)
        TT = ps("TT", 1024)
        OB = ps("OB", 512)

        s_w = sem("s_w")
        s_zero = sem("s_zero")
        s_cast = sem("s_cast")
        s_fold = sem("s_fold")
        s_hi = sem("s_hi")
        s_lo = sem("s_lo")
        s_tab = sem("s_tab")
        s_b1mm = sem("s_b1mm")
        s_b1 = sem("s_b1")
        s_qkvw = sem("s_qkvw")
        s_wow = sem("s_wow")
        s_ffnw = sem("s_ffnw")
        s_rope = sems("s_rope", TILES)
        s_x = sems("s_x", TILES)
        s_h = sems("s_h", 4)
        s_th = sem("s_th")
        s_hT = sem("s_hT")
        s_hl = sem("s_hl")
        s_q = sem("s_q")
        s_k = sem("s_k")
        s_v = sem("s_v")
        s_sq = sem("s_sq")
        s_vown = sem("s_vown")
        s_vlo = sems("s_vlo", 2)
        s_vup = sems("s_vup", 2)
        s_n2 = sem("s_n2")
        s_cl = sem("s_cl")
        s_rn = sem("s_rn")
        s_qg = sem("s_qg")
        s_rot = sem("s_rot")
        s_qr = sem("s_qr")
        s_ka = sem("s_ka")
        s_kr = sem("s_kr")
        s_tqk = sem("s_tqk")
        s_qT = sem("s_qT")
        s_kT = sem("s_kT")
        s_s = sem("s_s")
        s_mx = sem("s_mx")
        s_sh = sem("s_sh")
        s_p = sem("s_p")
        s_tp = sem("s_tp")
        s_pTv = sem("s_pTv")
        s_pTa = sem("s_pTa")
        s_o = sem("s_o")
        s_rsum = sem("s_rsum")
        s_on = sem("s_on")
        s_to = sem("s_to")
        s_oT = sem("s_oT")
        s_y = sem("s_y")
        s_xm = sem("s_xm")
        s_xb2 = sem("s_xb2")
        s_h2 = sems("s_h2", 4)
        s_st2 = sem("s_st2")
        s_mv2 = sem("s_mv2")
        s_ve2 = sem("s_ve2")
        s_rs2 = sem("s_rs2")
        s_h2n = sem("s_h2n")
        s_th2 = sem("s_th2")
        s_h2T = sem("s_h2T")
        s_h2l = sem("s_h2l")
        s_w1 = sem("s_w1")
        s_gelu = sem("s_gelu")
        s_act2 = sem("s_act2")
        s_w2 = sem("s_w2")
        s_xn = sem("s_xn")
        s_st = sem("s_st")
        g_in = sems("g_in", SEQS)
        g_fin = sems("g_fin", SEQS)
        g_ld = sem("g_ld")
        g_x1 = sem("g_x1")
        g_st = sem("g_st")
        g_mv = sem("g_mv")
        g_ve = sem("g_ve")
        g_rs = sem("g_rs")
        g_y = sem("g_y")
        g_xy = sem("g_xy")
        g_ty = sem("g_ty")
        g_yT = sem("g_yT")
        g_pr = sem("g_pr")
        g_z = sem("g_z")
        g_zn = sem("g_zn")
        g_vg = sem("g_vg")
        g_tk = sem("g_tk")
        g_kT = sem("g_kT")
        g_s = sem("g_s")
        g_mx = sem("g_mx")
        g_nm = sem("g_nm")
        g_p = sem("g_p")
        g_tp = sem("g_tp")
        g_pTv = sem("g_pTv")
        g_pTa = sem("g_pTa")
        g_o = sem("g_o")
        g_rl = sem("g_rl")
        g_x2 = sem("g_x2")
        g_sto = sem("g_sto")

        block = ctx.enter_context(nc.Block())

        arrived = (x_att, x_mid, x_b2, x_2)
        kept = (v_g, x_2, pT2, pT)
        half_step = (x_att, x_mid, x_b2, sq)

        y_in = gelu[:].rearrange("p a (t c) -> p (a t) c", c=DIM)

        rope_raw = probs[:].rearrange("p b h k -> p (b h k)")
        staged = act2[:].rearrange("p a b c -> p (a b c)")
        w_1raw = staged[:, 0:DEPTH * 2 * HID].rearrange("p (l n) -> p l n", l=DEPTH)
        w_1ln = staged[:, DEPTH * 2 * HID:2 * DEPTH * 2 * HID].rearrange("p (l n) -> p l n", l=DEPTH)
        own_cols, prev_cols = (buf[:].rearrange("p b n -> p (b n)") for buf in (v_own, v_prev))
        third = 3 * INNER
        qkv_raw = [own_cols[:, 0:third], prev_cols[:, 2 * INNER:2 * INNER + third]]
        rope_of = [(rope[:, 0:HALF].rearrange("p t a b d -> p t (a b d)"),
                    rope[:, HALF:TILES].rearrange("p t a b d -> p t (a b d)")),
                   tuple(buf[:].rearrange("p (t m) -> p t m", m=4 * DH) for buf in (rope_c, rope_s))]
        qkv_of = [(w_qkv[:, 0, :], w_qkv[:, 1, :]),
                  (own_cols[:, third:2 * third], prev_cols[:, 2 * INNER + third:2 * INNER + 2 * third])]
        w1_of = [(w_1[:, 0, :], w_1[:, 1, :]),
                 tuple(buf[:].rearrange("p b n -> p (b n)")[:, 0:2 * HID] for buf in (q_r, k_r))]
        y_T = q_r[:].rearrange("p b n -> p (b n)")

        def fr(ap):
            return ap.bitcast(F32R)

        def product(mm, dst, left, right):
            for k, (a, b) in enumerate(((0, 0), (0, 1), (1, 0))):
                last = mm(dst, fr(left(a)), fr(right(b)), start=(k == 0), stop=(k == 2))
            return last

        def flat(buf):
            return buf[:].rearrange("p t c -> p (t c)") if len(buf.shape) == 3 else buf[:]

        def tokens(buf):
            return buf[:] if len(buf.shape) == 3 else buf[:].rearrange("p (t c) -> p t c", t=TILES)

        def banks(k):
            src = TT if k % 2 == 0 else QK
            return src[:, 0:512], src[:, 512:1024]

        def qk(ap):
            return ap.rearrange("p (t h d) -> p t h d", t=2, d=DH)

        def rows(ap):
            return ap.rearrange("(t p) c -> p t c", p=P)

        def stack_done(eng, stack):
            eng.wait_ge(s_st, (stack + 1) * ITERS * 32 + 16)

        @block.sync
        def _(sp):
            for s in range(SEQS):
                sp.dma_start(arrived[s][:], rows(x_in[s])).then_inc(g_in[s], 16)
            for dst, src in ((rope_raw, rope_in.rearrange("p t a b d -> p (t a b d)")), (qkv_raw[0], wqkv[0]),
                             (qkv_raw[1], wqkv[1]), (ident[:], ident_in), (mask_f[:], mask_in),
                             (w_1raw, w1_in.rearrange("l c n -> c l n")),
                             (w_kqv[:], w_attn), (kq_gb[:], kq_gain), (ln_gb_sb[:], ln_gb),
                             (b_kqv[:], b_attn.partition_broadcast(P)),
                             (v_gb[:], v_gain.partition_broadcast(P)),
                             (b_2all[:], b2_in.partition_broadcast(P)),
                             (gains[:, :, :, 0, :], qk_gain.partition_broadcast(P)),
                             (gains[:, :, :, 1, 0:32], qk_gain[:, :, 32:64].partition_broadcast(P)),
                             (gains[:, :, :, 1, 32:64], qk_gain[:, :, 0:32].partition_broadcast(P))):
                sp.dma_start(dst, src).then_inc(s_w, 16)
            sp.dma_start(b_1raw[:], b1_in).then_inc(s_w, 16)
            sp.wait_ge(s_zero, ZEROED)
            sp.dma_start(stream[:, :, 0, :].rearrange("l s c -> (l s) c"), zeros[0:(DEPTH + 1) * SEQS, :]).then_inc(s_st, 16)

            def store_tables(l):
                for part in range(2):
                    sp.dma_start(rope_d[l, :, part * HALF:part * HALF + HALF].rearrange("p t a b d -> p t (a b d)"),
                                 rope_of[l][part]).then_inc(s_tab, 16)
                    sp.dma_start(qkv_d[l, :, part], qkv_of[l][part]).then_inc(s_tab, 16)
                    sp.dma_start(w1_d[l, :, part], w1_of[l][part]).then_inc(s_tab, 16)

            def load_rope(l, i):
                sp.dma_start(rope[:, i], rope_d[l, :, i]).then_inc(s_rope[i], 16)

            def load_ffn(l, whole=True):
                if whole:
                    sp.dma_start(w_1[:], w1_d[l]).then_inc(s_ffnw, 16)
                sp.dma_start(b_1[:], b_1all[:, l]).then_inc(s_ffnw, 16)
                sp.dma_start(b_2[:], b_2all[:, l]).then_inc(s_ffnw, 16)
                for c, (at, n) in enumerate(CH):
                    sp.dma_start(w_2[0:n, c, :], w2_in[l, at:at + n, :]).then_inc(s_ffnw, 16)

            def load_qkv(l):
                sp.dma_start(w_qkv[:], qkv_d[l]).then_inc(s_qkvw, 16)

            def load_wo(l):
                sp.dma_start(w_o[:], wo_in[l].rearrange("(c p) n -> p c n", p=P)).then_inc(s_wow, 16)

            def loads(t, l, s):
                i, k = t.i, t.i % 4
                base = P * i
                sp.dma_start(x_att[:, i, :], stream[l, s, base + 1:base + 1 + P, :]).then_inc(s_x[i], 16)
                sp.dma_start(h[:, k, 0:64], stream[l, s, base + 1:base + 1 + P, 0:64]).then_inc(s_h[k], 16)
                sp.dma_start(h[:, k, 64:128], stream[l, s, base:base + P, 64:128]).then_inc(s_h[k], 16)

            def moves(tile):
                if t := tile(QKV):
                    a, k = t.i % 2, t.i
                    need(sp, s_vown, t.count())
                    sp.dma_start(v_prev[0:64, k, :], v_own[0:64, k, :]).then_inc(s_vlo[a], 16)
                    sp.dma_start(v_prev[64:128, (k + 1) % TILES, :], v_own[64:128, k, :]).then_inc(s_vup[a], 16)
                if t := tile(WO):
                    i, k = t.i, t.i % 4
                    need(sp, s_xm, t.count())
                    sp.dma_start(h2[:, k, 0:64], x_mid[:, i, 0:64]).then_inc(s_h2[k], 16)
                    sp.dma_start(h2[1:128, k, 64:128], x_mid[0:127, i, 64:128]).then_inc(s_h2[k], 16)
                    before = x_mid[127:128, i - 1, 64:128] if i else zeros[0:1, 0:64]
                    sp.dma_start(h2[0:1, k, 64:128], before).then_inc(s_h2[k], 16)

            def store(l, s, n):
                for half in range(2):
                    need(sp, s_xn, n * 2 + (half + 1))
                    a, b = half * HALF, (half + 1) * HALF
                    sp.dma_start(rows(stream[l + 1, s, 1 + a * P:1 + b * P, :]), x_new[:, a:b, :]).then_inc(s_st, 16)

            def stack(k):
                first = k * ITERS

                def iteration(it, c, l, s, lb, sb_, at=(), after_burst=None):
                    for j in range(TILES):
                        def tile(skew):
                            n = j - skew + c
                            return Tile(it, n, k) if it is not None or 0 <= n < NT else None
                        if l is not None:
                            if not isinstance(l, int) or l > 0:
                                if j == 0:
                                    need(sp, s_st, (first - 1 + (c // TILES if it is None else it)) * 32 + 16)
                            loads(tile(0), l, s)
                        for when, do in at:
                            if when == j:
                                do()
                        moves(tile)
                        if j == BURST - TILES and lb is not None:
                            store(lb, sb_, (c // TILES if it is None else it) - 1 + first)
                            if after_burst:
                                after_burst()

                def wait_tile(s_, n, unit=1):
                    need(sp, s_, (n + k * NT + 1) * unit)

                if k == 0:
                    load_wo(0)
                    for s in range(SEQS):
                        sp.wait_ge(g_y, s + 1)
                        sp.dma_start(rows(stream[0, s, 1:, :]), arrived[s][:]).then_inc(g_sto, 16)
                    sp.wait_ge(s_lo, 4)
                    store_tables(1)
                    sp.wait_ge(s_w, N_CONST)
                    sp.wait_ge(s_b1, 1)
                    load_ffn(0, whole=False)
                    sp.wait_ge(g_sto, 16 * SEQS)
                    sp.wait_ge(s_st, 16)
                iteration(None, 0, 0, 0, None, None)
                if k == 0:
                    sp.wait_ge(s_rope[TILES - 1], 1)
                    sp.wait_ge(s_qkvw, 1)
                    sp.wait_ge(s_ffnw, 96 - 15)
                    store_tables(0)
                with sp.Fori(1, SEQS - 1) as it:
                    iteration(it, 0, 0, it, 0, it - 1)
                sp.wait_ge(s_tab, DEPTH * 6 * 16)
                m = (SEQS - 1) * TILES

                def rope_after(i):
                    def do():
                        wait_tile(s_rot, m + i)
                        load_rope(1, i)
                    return do

                iteration(None, m, 0, SEQS - 1, 0, SEQS - 2,
                          [(i + 3, rope_after(i)) for i in range(TILES - 3)])

                def after_qkv():
                    wait_tile(s_v, m + TILES - 1)
                    load_qkv(1)

                def after_wo():
                    wait_tile(s_y, m + TILES - 1)
                    load_wo(1)

                iteration(None, m + TILES, 1, 0, 0, SEQS - 1,
                          [(0, rope_after(5)), (1, rope_after(6)), (2, after_qkv), (2, rope_after(7)), (6, after_wo)],
                          lambda: load_ffn(1))
                with sp.Fori(SEQS + 1, ITERS) as it:
                    iteration(it, 0, 1, it - SEQS, 1, it - SEQS - 1)
                for g in range(NT, LAST + 1):
                    moves(lambda skew: Tile(None, g - skew, k) if 0 <= g - skew < NT else None)
                store(1, SEQS - 1, first + ITERS - 1)

            stack(0)
            stack_done(sp, 0)

            def attention_loads(s):
                sp.dma_start(x_att[:], rows(x_in[s])).then_inc(g_ld, 16)
                sp.dma_start(x_b2[:], rows(stream[DEPTH, s, 1:, :])).then_inc(g_ld, 16)

            def attention(s, more):
                if more:
                    sp.wait_ge(g_x1, s + 1)
                    attention_loads(s + 1)
                sp.wait_ge(g_x2, (s + 1) * TILES)
                sp.dma_start(rows(mid[s]), x_2[:]).then_inc(g_sto, 16)
                sp.wait_ge(g_y, s * 2 + (SEQS + 2))
                sp.dma_start(rows(stream[0, s, 1:, :]), x_new[:]).then_inc(g_sto, 16)

            attention_loads(0)
            load_qkv(0)
            load_wo(0)
            for i in range(TILES):
                load_rope(0, i)
            load_ffn(0)
            with sp.Fori(0, SEQS - 1) as s:
                attention(s, True)
            attention(SEQS - 1, False)
            sp.wait_ge(g_sto, SEQS * 3 * 16)
            for s in range(SEQS - 1):
                sp.dma_start(tokens(kept[s]), rows(mid[s])).then_inc(g_fin[s], 16)
            stack(1)
            stack_done(sp, 1)
            sp.dma_start(tokens(kept[SEQS - 1]), rows(mid[SEQS - 1])).then_inc(g_fin[SEQS - 1], 16)
            for s in range(SEQS):
                sp.dma_start(tokens(half_step[s]), rows(stream[DEPTH, s, 1:, :])).then_inc(g_fin[s], 16)
            for s in range(SEQS):
                sp.wait_ge(g_x2, SEQS * TILES + s + 1)
                sp.dma_start(rows(out[s]), tokens(kept[s])).then_inc(g_sto, 16)
            sp.wait_ge(g_sto, SEQS * 4 * 16)

        @block.tensor
        def _(pe):
            mm = nc.tensor.matmul

            def transpose(dst, src):
                return nc.tensor.transpose(dst, src, ident[:])

            pe.wait_ge(s_w, N_CONST)
            pe.wait_ge(s_cast, 2)
            for l in range(DEPTH):
                for g in range(2):
                    for c, (at, n) in enumerate(CH):
                        k = (l * 2 + g) * 3 + c
                        last = mm(VB[0:n, k:k + 1], w_1raw[:, l, g * HID + at:g * HID + at + n],
                                  ln_gb_sb[:, 1, l:l + 1], start=True, stop=True)
            last.then_inc(s_b1mm, 1)
            pe.wait_ge(s_b1, 1)

            def probs_transposed(t, half):
                pe.wait_ge(s_p, t.count(unit=2) + (half - 1))
                for hd in range(4 * half, 4 * half + 4):
                    last = transpose(TT[:, hd * P:hd * P + P], probs[:, t.i % 2, hd, :])
                last.then_inc(s_tp, 1)

            def masked(t, bank):
                m = 1 if t.i == 0 else 0
                mm(SC[:, bank * 512:bank * 512 + 512], ident_b[:],
                   mask_b[:, m:m + 1, :].to_broadcast([P, 4, P]), start=True, stop=False,
                   skip_group_check=True)

            def scored(t, half):
                i, b = t.i, t.i % 2
                sc = SC[:, :].rearrange("q (c e b k) -> q c e b k", c=PAIRS, e=2, b=2)
                chunks = (2 * half, 2 * half + 1)
                for c in chunks:
                    last = mm(sc[:, c, :, 0, :], qT[:, b, c, :], kT[:, b, c, :, 0:64],
                              start=False, stop=True, skip_group_check=True)
                for c in chunks:
                    if i:
                        last = mm(sc[0:64, c, :, 1, :], qT[:, b, c, 0:64], kT[:, 1 - b, c, :, 64:128],
                                  start=False, stop=True, skip_group_check=True)
                for c in chunks:
                    last = mm(sc[64:128, c, :, 1, :], qT[:, b, c, 64:128], kT[:, b, c, :, 64:128],
                              start=False, stop=True, skip_group_check=True)
                last.then_inc(s_s, 1)

            def step(stack):
                def f(tile, burst, before):
                    if t := tile(TQK):
                        b = t.i % 2
                        pe.wait_ge(s_qr, t.count())
                        pe.wait_ge(s_kr, t.count())
                        if t2 := tile(QKV + 1):
                            pe.wait_ge(s_rot, t2.count())
                            pe.wait_ge(s_sq, t2.count())
                        for m, src in ((1, k_r), (0, q_r)):
                            for c in range(PAIRS):
                                last = transpose(QK[:, m * 512 + c * P:m * 512 + c * P + P], src[:, b, c * P:c * P + P])
                            last.then_inc(s_tqk, 1)
                    if t := tile(ATT):
                        probs_transposed(t, 0)
                    if t := tile(WO):
                        if t.i == 0:
                            pe.wait_ge(s_wow, t.loads() * 16)
                        pe.wait_ge(s_oT, t.count())
                        if before is not None:
                            pe.wait_ge(s_xn, before * 2 + 2)
                        for c in range(PAIRS):
                            last = mm(OB[:, 0:DIM], oT[:, c, :], w_o[:, c, :], start=(c == 0), stop=(c == PAIRS - 1))
                        last.then_inc(s_y, 1)
                    if t := tile(QKV):
                        i, b = t.i, t.i % 2
                        if i == 0:
                            pe.wait_ge(s_qkvw, t.loads() * 16 - 15)
                        pe.wait_ge(s_hl, t.count())
                        if t2 := tile(TQK):
                            pe.wait_ge(s_qT, t2.count())
                            pe.wait_ge(s_kT, t2.count())
                        else:
                            need(pe, s_rot, t.count(back=1))
                            need(pe, s_sq, t.count(back=1))
                        for m, signal in ((0, s_q), (1, s_k)):
                            product(mm, QK[:, m * 512:m * 512 + 512], lambda x: hT[:, b, x, :],
                                    lambda x: w_qkv[:, x, m * 512:m * 512 + 512]).then_inc(signal, 1)
                        if t2 := tile(FFN_IN + 1):
                            pe.wait_ge(s_h2l, t2.count())
                        if before is not None:
                            pe.wait_ge(s_xn, before * 2 + 1)
                        product(mm, VB[:], lambda x: hT[:, b, x, :], lambda x: w_qkv[:, x, 1024:1536]).then_inc(s_v, 1)
                    if t := tile(ATT):
                        b = t.i % 2
                        pe.wait_ge(s_vlo[b], t.count(every=2, unit=16))
                        if t.it is not None or t.c > 0:
                            pe.wait_ge(s_vup[1 - b], t.count(back=1, every=2, unit=16))
                        probs_transposed(t, 1)
                    if t := tile(TQK):
                        need(pe, s_p, t.count(back=1, unit=2))
                        masked(t, 0)
                        masked(t, 1)
                        pe.wait_ge(s_qT, t.count())
                        pe.wait_ge(s_kT, t.count())
                        scored(t, 0)
                    if t := tile(ATT):
                        b = t.i % 2
                        pe.wait_ge(s_pTv, t.count())
                        pe.wait_ge(s_pTa, t.count())
                        need(pe, s_xm, t.count(back=1))
                        for w, v in ((0, v_prev), (1, v_own)):
                            for hd in range(HEADS):
                                last = mm(OB[64 * w:64 * w + 64, hd * DH:hd * DH + DH],
                                          pT[:, hd, 64 * w:64 * w + 64], v[:, t.i, hd * DH:hd * DH + DH],
                                          start=True, stop=True)
                        last.then_inc(s_o, 1)
                    if t := tile(TQK):
                        scored(t, 1)
                    if t := tile(TH):
                        pe.wait_ge(s_h[t.i % 4], t.count(every=4, unit=32))
                        need(pe, s_vown, t.count(back=1))
                        need(pe, s_hl, t.count(back=1))
                        transpose(VB[:, 0:P], h[:, t.i % 4, :]).then_inc(s_th, 1)
                    if t := tile(FFN_IN):
                        pe.wait_ge(s_h2n, t.count())
                        if t2 := tile(QKV):
                            pe.wait_ge(s_vown, t2.count())
                        else:
                            pe.wait_ge(s_h2l, t.count(back=1))
                        transpose(VB[:, P:2 * P], h2n[:, t.i % 2, :]).then_inc(s_th2, 1)
                    if t := tile(ATT):
                        pe.wait_ge(s_on, t.count())
                        for c in range(PAIRS):
                            last = transpose(OB[:, c * P:c * P + P], o_n[:, c * P:c * P + P])
                        last.then_inc(s_to, 1)
                    if burst is not None:
                        ffn(tile, burst)
                return f

            def ffn(tile, n):
                last_in = tile(FFN_IN)
                pe.wait_ge(s_ffnw, last_in.loads() * 96 - 15)

                def w1_pair(k):
                    half, c = divmod(k, 3)
                    at, m = CH[c]
                    a, g = banks(k)
                    if k >= 2:
                        pe.wait_ge(s_act2, n * 6 + (k - 1))
                    if k == 1 and (t := tile(QKV)):
                        pe.wait_ge(s_rot, t.count())
                        pe.wait_ge(s_sq, t.count())
                    if k == 3:
                        pe.wait_ge(s_h2l, last_in.count())
                    for dst, col in ((g, HID + at), (a, at)):
                        product(mm, dst[0:m], lambda x: w_1[:, x, col:col + m],
                                lambda x: h2T[:, x, half * 512:half * 512 + 512]).then_inc(s_w1, 1)

                def w2_half(half):
                    dst = VB if half == 0 else OB
                    pe.wait_ge(s_act2, n * 6 + (3 * half + 3))
                    if half == 0:
                        if t := tile(TH):
                            pe.wait_ge(s_hl, t.count())
                    elif t := tile(ATT):
                        pe.wait_ge(s_oT, t.count())
                    for q in range(HALF):
                        for c, (at, m) in enumerate(CH):
                            last = mm(dst[:, q * DIM:q * DIM + DIM], act2[0:m, half, c, q * P:q * P + P],
                                      w_2[0:m, c, :], start=(c == 0), stop=(c == 2))
                    last.then_inc(s_w2, 1)

                for k in range(6):
                    w1_pair(k)
                w2_half(0)
                w2_half(1)

            pipeline(pe, step(0), 0)
            stack_done(pe, 0)

            with pe.Fori(0, SEQS) as s:
                pe.wait_ge(g_y, s * 2 + (SEQS + 1))
                for i in range(TILES):
                    last = transpose(TT[:, i * P:i * P + P], y_in[:, i, :])
                last.then_inc(g_ty, 1)
                pe.wait_ge(g_yT, s + 1)
                for i in range(TILES):
                    if i >= 2:
                        pe.wait_ge(g_z, s * TILES + (i - 1))
                    mm(QK[:, i % 2 * 512:i % 2 * 512 + 384], y_T[:, i * P:i * P + P],
                       w_kqv[:, :, :].rearrange("p a b -> p (a b)"), start=True, stop=True).then_inc(g_pr, 1)
                zn = act2[:].rearrange("p a b c -> p (a b c)").rearrange("p (i m) -> p i m", i=TILES)
                for m, dst in ((0, TT), (1, SC)):
                    pe.wait_ge(g_zn, s * 3 + (m + 1))
                    for i in range(TILES):
                        last = transpose(dst[:, i * P:i * P + P], zn[:, i, m * DIM:m * DIM + DIM])
                    last.then_inc(g_tk, 1)
                pe.wait_ge(g_kT, s * 2 + 2)
                for i in range(TILES + 2):
                    if i < TILES:
                        dst = QK if i % 2 else SC
                        if i >= 2:
                            pe.wait_ge(g_p, s * TILES + (i - 1))
                        for m in range(2):
                            last = mm(dst[:, m * 512:m * 512 + 512], rope_c[:, i * P:i * P + P],
                                      rope_s[:, m * 512:m * 512 + 512], start=True, stop=True)
                        last.then_inc(g_s, 1)
                    if 0 <= (k := i - 1) < TILES:
                        pe.wait_ge(g_p, s * TILES + (k + 1))
                        if k:
                            pe.wait_ge(g_pTv, s * TILES + k)
                            pe.wait_ge(g_pTa, s * TILES + k)
                        for m in range(TILES):
                            last = transpose(TT[:, m * P:m * P + P], probs[:, k % 2, m, :])
                        last.then_inc(g_tp, 1)
                    if 0 <= (k := i - 2):
                        pe.wait_ge(g_pTv, s * TILES + (k + 1))
                        pe.wait_ge(g_pTa, s * TILES + (k + 1))
                        if k >= 2:
                            pe.wait_ge(g_x2, s * TILES + (k - 1))
                        if k == 0:
                            pe.wait_ge(g_vg, s * 2 + 2)
                        dst = OB if k % 2 else VB
                        src = pT2 if k % 2 else pT
                        for m in range(TILES):
                            last = mm(dst[:, 0:DIM], src[:, m, :], v_g[:, m, :], start=(m == 0), stop=(m == TILES - 1))
                        last.then_inc(g_o, 1)
                pe.wait_ge(g_x2, s * TILES + TILES)

            pipeline(pe, step(1), 1)

        @block.vector
        def _(dve):
            v = nc.vector
            v.memset(zeros[:], 0.0).then_inc(s_zero, 1)
            v.memset(kT[:], 0.0).then_inc(s_zero, 1)
            v.memset(v_prev[:, 0, :], 0.0).then_inc(s_zero, 1)
            v.memset(b_1all[:], 0.0).then_inc(s_zero, 1)
            v.memset(mhalf[:], -0.5).then_inc(s_zero, 1)
            v.memset(epsilon[:], EPS).then_inc(s_zero, 1)
            def stats(tile, slot):
                return v.bn_stats(st_g[:, slot, :], tile)

            def stats_fence(n):
                dve.wait_ge(g_st, n * 2 - 1)
                v.tensor_copy(fence[:], zeros[:, 0:1]).then_inc(g_st, 1)

            def aggregate(n, slot):
                for k in range(slot, slot + n):
                    last = v.bn_aggr(mv_g[:, k, :], st_g[:, k, :])
                last.then_inc(g_mv, 1)

            def normalise(dst, src, slot):
                for k in range(TILES):
                    m = slot + k
                    last = v.tensor_scalar(dst[:, k, :], src[:, k, :], mv_g[:, m, 0:1], rs_g[:, m:m + 1],
                                           ALU.subtract, ALU.mult)
                return last

            dve.wait_ge(s_zero, ZEROED)
            for s in range(SEQS):
                dve.wait_ge(g_in[s], 16)
                for k in range(TILES):
                    last = stats(arrived[s][:, k, :], s * TILES + k)
                last.then_inc(g_st, 1)
                stats_fence(s + 1)
                aggregate(TILES, s * TILES)
            for s in range(SEQS):
                dve.wait_ge(g_rs, s + 1)
                normalise(arrived[s], arrived[s], s * TILES).then_inc(g_y, 1)
            dve.wait_ge(s_w, N_CONST)
            v.tensor_copy(ident_b[:], ident[:]).then_inc(s_cast, 1)
            v.tensor_copy(mask_b[:], mask_f[:]).then_inc(s_cast, 1)
            def rotation(l, i, n):
                at = i % HALF
                return v.tensor_tensor(rope_of[l][i // HALF][:, at:at + n], rope_raw.rearrange("p (t m) -> p t m", t=TILES)[:, i:i + n],
                                       gains[:, l].rearrange("p a b d -> p (a b d)").unsqueeze(1).to_broadcast([P, n, 4 * DH]),
                                       ALU.mult)

            for l in (1, 0):
                if l:
                    for i in (0, HALF):
                        rotation(l, i, HALF).then_inc(s_lo, 1)
                else:
                    for i in range(TILES):
                        rotation(l, i, 1).then_inc(s_rope[i], 1)
                done = 2 * (1 - l)
                dve.wait_ge(s_hi, done + 1)
                hi, lo = qkv_of[l]
                v.tensor_tensor(fr(lo), qkv_raw[l], hi, ALU.subtract).then_inc(*((s_lo, 1) if l else (s_qkvw, 1)))
                dve.wait_ge(s_hi, done + 2)
                hi, lo = w1_of[l]
                v.tensor_tensor(fr(lo), w_1ln[:, l, :], hi, ALU.subtract).then_inc(*((s_lo, 1) if l else (s_ffnw, 1)))
            dve.wait_ge(s_b1mm, 1)
            for l in range(DEPTH):
                for c in range(6):
                    n = CH[c % 3][1]
                    k = l * 6 + c
                    last = v.tensor_tensor(b_1all[0:n, l, c:c + 1], VB[0:n, k:k + 1], b_1raw[0:n, l, c:c + 1], ALU.add)
            last.then_inc(s_b1, 1)

            def highest(t, half):
                dve.wait_ge(s_s, t.count(unit=2) + (half - 1))
                v.tensor_reduce(top[:, t.i % 2, 4 * half:4 * half + 4],
                                SC[:, half * 512:half * 512 + 512].rearrange("q (h k) -> q h k", h=4),
                                AX, ALU.max).then_inc(s_mx, 1)

            def shifted(t, half):
                hd = slice(4 * half, 4 * half + 4)
                dve.wait_ge(s_mx, t.count(unit=2) + (half - 1))
                v.scalar_tensor_tensor(out=shift[:, t.i % 2, hd], in0=top[:, t.i % 2, hd], scalar=-1.0,
                                       in1=qgain[:, t.i % 2, hd], op0=ALU.mult, op1=ALU.mult).then_inc(s_sh, 1)

            def clipped(t):
                b = t.i % 2
                dve.wait_ge(s_n2, t.count())
                v.tensor_scalar(clip2[:, b, 8:16], norm2[:, b, 8:16], 1e-24, None, ALU.max).then_inc(s_cl, 1)
                need(dve, s_qg, t.count(back=2))
                v.tensor_scalar(clip2[:, b, 0:8], norm2[:, b, 0:8], 1e-24, QK_SCALE ** -2,
                                ALU.max, ALU.mult).then_inc(s_cl, 1)

            def step(tile, burst, before):
                if before is not None:
                    for half in range(2):
                        dve.wait_ge(s_w2, before * 2 + (half + 1))
                        if half == 0:
                            dve.wait_ge(s_xb2, tile(FFN_IN + 1).count())
                            dve.wait_ge(s_st, before * 32 + 16)
                        src = (VB if half == 0 else OB)[:, :].rearrange("p (t c) -> p t c", t=HALF)
                        v.tensor_tensor(x_new[:, half * HALF:half * HALF + HALF, :], src,
                                        x_b2[:, half * HALF:half * HALF + HALF, :], ALU.add).then_inc(s_xn, 1)
                if t := tile(QKV + 1):
                    clipped(t)
                if t := tile(FFN_IN):
                    b, k = t.i % 2, t.i % 4
                    dve.wait_ge(s_h2[k], t.count(every=4, unit=48))
                    v.bn_stats(st2[:, b, :], h2[:, k, :]).then_inc(s_st2, 1)
                if t := tile(ATT):
                    dve.wait_ge(s_tp, t.count(unit=2) - 1)
                    need(dve, s_o, t.count(back=1))
                    v.tensor_copy(pT[:, 0:4, :], TT[:, 0:512].rearrange("k (h q) -> k h q", h=4)).then_inc(s_pTv, 1)
                if t := tile(WO):
                    i = t.i
                    if t2 := tile(FFN_IN):
                        dve.wait_ge(s_st2, t2.count())
                    dve.wait_ge(s_y, t.count())
                    dve.wait_ge(s_x[i], t.count(every=TILES, unit=16))
                    need(dve, s_xb2, t.count(back=2))
                    v.tensor_tensor(x_mid[:, i, :], OB[:, 0:DIM], x_att[:, i, :], ALU.add).then_inc(s_xm, 1)
                if t := tile(FFN_IN):
                    if not tile(WO):
                        dve.wait_ge(s_st2, t.count())
                    v.bn_aggr(mv2[:, t.i % 2, :], st2[:, t.i % 2, :]).then_inc(s_mv2, 1)
                if t := tile(QKV):
                    i = t.i
                    dve.wait_ge(s_rope[i], t.loads() * 16 - 15)
                    need(dve, s_qr, t.count(back=1))
                    need(dve, s_ka, t.count(back=1))
                    for m, signal in ((0, s_q), (1, s_k)):
                        dve.wait_ge(signal, t.count())
                        src = qk(QK[:, :])[:, m]
                        v.tensor_tensor(qk(rope_c[:])[:, m], src,
                                        rope[:, i, m, 0:1, :].to_broadcast([P, HEADS, DH]), ALU.mult)
                        sin = rope[:, i, m, 1:2, :]
                        for half in range(2):
                            a, o = 32 * half, 32 * (1 - half)
                            last = v.tensor_tensor(qk(rope_s[:])[:, m, :, a:a + 32], src[:, :, o:o + 32],
                                                   sin[:, :, a:a + 32].to_broadcast([P, HEADS, 32]), ALU.mult)
                    last.then_inc(s_rot, 1)
                if t := tile(FFN_IN):
                    b, k = t.i % 2, t.i % 4
                    dve.wait_ge(s_rs2, t.count())
                    need(dve, s_th2, t.count(back=2))
                    v.tensor_scalar(h2n[:, b, :], h2[:, k, :], mv2[:, b, 0:1], rstd2[:, b, :],
                                    ALU.subtract, ALU.mult).then_inc(s_h2n, 1)
                if t := tile(ATT):
                    b = t.i % 2
                    dve.wait_ge(s_p, t.count(unit=2))
                    v.reciprocal(rsums[:, b, :], psums[:, b, :]).then_inc(s_rsum, 1)
                if t := tile(TQK):
                    need(dve, s_p, t.count(back=2, unit=2))
                    dve.wait_ge(s_qg, t.count())
                    highest(t, 0)
                    shifted(t, 0)
                if t := tile(ATT):
                    b = t.i % 2
                    dve.wait_ge(s_rsum, t.count())
                    dve.wait_ge(s_o, t.count())
                    need(dve, s_to, t.count(back=1))
                    v.tensor_tensor(o_n[:].rearrange("q (h d) -> q h d", h=HEADS),
                                    OB[:, :].rearrange("q (h d) -> q h d", h=HEADS),
                                    rsums[:, b, :].unsqueeze(2).to_broadcast([P, HEADS, DH]), ALU.mult).then_inc(s_on, 1)
                if t := tile(TQK):
                    highest(t, 1)
                    shifted(t, 1)
                if t := tile(QKV):
                    b = t.i % 2
                    dve.wait_ge(s_sq, t.count())
                    need(dve, s_rn, t.count(back=2))
                    v.tensor_reduce(norm2[:, b, :], sq[:].rearrange("p (h d) -> p h d", d=DH), AX, ALU.add).then_inc(s_n2, 1)
                if t := tile(TH):
                    b = t.i % 2
                    dve.wait_ge(s_hT, t.count())
                    if t2 := tile(FFN_IN):
                        dve.wait_ge(s_h2T, t2.count())
                    need(dve, s_v, t.count(back=2))
                    v.tensor_tensor(fr(hT[:, b, 1, :]), VB[:, 0:P], hT[:, b, 0, :], ALU.subtract).then_inc(s_hl, 1)
                if t := tile(FFN_IN):
                    dve.wait_ge(s_h2T, t.count())
                    own = slice(t.i * P, t.i * P + P)
                    v.tensor_tensor(fr(h2T[:, 1, own]), VB[:, P:2 * P], h2T[:, 0, own], ALU.subtract).then_inc(s_h2l, 1)
                if burst is not None:
                    n = burst
                    for k in range(6):
                        half, c = divmod(k, 3)
                        m = CH[c][1]
                        dve.wait_ge(s_gelu, n * 6 + (k + 1))
                        dve.wait_ge(s_w1, n * 12 + (2 * k + 2))
                        v.scalar_tensor_tensor(out=act2[0:m, half, c, :], in0=banks(k)[0][0:m], scalar=b_1[0:m, c:c + 1],
                                               in1=gelu[0:m, k % 2, :], op0=ALU.add, op1=ALU.mult).then_inc(s_act2, 1)

            pipeline(dve, step, 0)
            stack_done(dve, 0)

            with dve.Fori(0, SEQS) as s:
                lot, rs = s * 3 + SEQS, s * 5 + SEQS
                dve.wait_ge(g_ld, s * 32 + 32)
                v.scalar_tensor_tensor(out=flat(x_mid), in0=flat(x_b2), scalar=0.5, in1=flat(x_att),
                                       op0=ALU.mult, op1=ALU.add).then_inc(g_x1, 1)
                dve.wait_ge(g_x1, s + 1)
                for k in range(TILES):
                    last = stats(x_mid[:, k, :], LN_IN + k)
                last.then_inc(g_st, 1)
                stats_fence(lot + 1)
                aggregate(TILES, LN_IN)
                dve.wait_ge(g_rs, rs + 1)
                normalise(y_in, x_mid, LN_IN).then_inc(g_y, 1)
                z = act2[:].rearrange("p a b c -> p (a b c)").rearrange("p (i m) -> p i m", i=TILES)
                for i in range(TILES + 1):
                    if i < TILES:
                        dve.wait_ge(g_pr, s * TILES + (i + 1))
                        v.tensor_tensor(z[:, i, :], QK[:, i % 2 * 512:i % 2 * 512 + 384], b_kqv[:], ALU.add).then_inc(g_z, 1)
                    if i:
                        dve.wait_ge(g_z, s * TILES + i)
                        for m in range(3):
                            last = stats(z[:, i - 1, m * DIM:m * DIM + DIM], KQV + m * TILES + i - 1)
                last.then_inc(g_st, 1)
                stats_fence(lot + 2)
                for m in range(3):
                    aggregate(TILES, KQV + m * TILES)
                for m in range(3):
                    dve.wait_ge(g_rs, rs + (m + 2))
                    zz = z[:, :, m * DIM:m * DIM + DIM]
                    normalise(zz, zz, KQV + m * TILES).then_inc(g_zn, 1)
                dve.wait_ge(g_sto, (s * 2 + SEQS) * 16)
                for i in range(TILES + 2):
                    if i < TILES:
                        b = i % 2
                        dve.wait_ge(g_s, s * TILES + (i + 1))
                        v.tensor_reduce(mx_g[:, b:b + 1], (QK if b else SC)[:, :], AX, ALU.max).then_inc(g_mx, 1)
                        dve.wait_ge(g_mx, s * TILES + (i + 1))
                        v.tensor_scalar(nm_g[:, b:b + 1], mx_g[:, b:b + 1], -1.0, None, ALU.mult).then_inc(g_nm, 1)
                    if 0 <= (k := i - 1) < TILES:
                        b = k % 2
                        dve.wait_ge(g_tp, s * TILES + (k + 1))
                        if k >= 2:
                            dve.wait_ge(g_o, s * TILES + (k - 1))
                        v.tensor_copy((pT2 if b else pT)[:, 0:4, :],
                                      TT[:, 0:512].rearrange("k (h q) -> k h q", h=4)).then_inc(g_pTv, 1)
                        if k >= 2:
                            dve.wait_ge(g_x2, s * TILES + (k - 1))
                        v.reciprocal(rl_g[:, b:b + 1], sm_g[:, b:b + 1]).then_inc(g_rl, 1)
                    if 0 <= (k := i - 2):
                        b = k % 2
                        dve.wait_ge(g_rl, s * TILES + (k + 1))
                        dve.wait_ge(g_o, s * TILES + (k + 1))
                        if k == 0:
                            dve.wait_ge(g_xy, s + 1)
                        v.scalar_tensor_tensor(out=x_2[:, k, :], in0=(OB if b else VB)[:, 0:DIM], scalar=rl_g[:, b:b + 1],
                                               in1=sq[:, k * DIM:k * DIM + DIM], op0=ALU.mult, op1=ALU.add).then_inc(g_x2, 1)
                        if k:
                            dve.wait_ge(g_x2, s * TILES + k)
                            stats(x_2[:, k - 1, :], LN_OUT + k - 1)
                dve.wait_ge(g_x2, s * TILES + TILES)
                stats(x_2[:, TILES - 1, :], LN_OUT + TILES - 1).then_inc(g_st, 1)
                stats_fence(lot + 3)
                aggregate(TILES, LN_OUT)
                dve.wait_ge(g_rs, rs + 5)
                normalise(x_new, x_2, LN_OUT).then_inc(g_y, 1)

            pipeline(dve, step, 1)
            for s in range(SEQS):
                dve.wait_ge(g_fin[s], 32)
                v.scalar_tensor_tensor(out=flat(kept[s]), in0=flat(half_step[s]), scalar=0.5, in1=flat(kept[s]),
                                       op0=ALU.mult, op1=ALU.add).then_inc(g_x2, 1)

        @block.scalar
        def _(act):
            def copy(dst, src):
                return nc.scalar.activation(dst, src, ACT.Copy)

            def exponentials(t, half):
                b = t.i % 2
                act.wait_ge(s_sh, t.count(unit=2) + (half - 1))
                for hd in range(4 * half, 4 * half + 4):
                    last = nc.scalar.activation(probs[:, b, hd, :], SC[:, hd * P:hd * P + P], ACT.Exp,
                                                bias=shift[:, b, hd:hd + 1], scale=qgain[:, b, hd:hd + 1],
                                                accum_out=psums[:, b, hd:hd + 1])
                last.then_inc(s_p, 1)

            def step(tile, burst, before):
                if t := tile(TQK):
                    b = t.i % 2
                    act.wait_ge(s_tqk, t.count(unit=2) - 1)
                    need(act, s_s, t.count(back=1, unit=2))
                    for e in range(2):
                        last = copy(kT[64 * e:64 * e + 64, b, :, e, :],
                                    QK[64 * e:64 * e + 64, 512:1024].rearrange("d (c t) -> d c t", c=PAIRS))
                    last.then_inc(s_kT, 1)
                    act.wait_ge(s_tqk, t.count(unit=2))
                    copy(qT[:, b], QK[:, 0:512].rearrange("d (c t) -> d c t", c=PAIRS)).then_inc(s_qT, 1)
                if t := tile(ATT):
                    exponentials(t, 1)
                if t := tile(QKV):
                    b = t.i % 2
                    act.wait_ge(s_v, t.count())
                    need(act, s_o, t.count(back=TILES - 1))
                    if t.it is not None or t.c >= 2:
                        act.wait_ge(s_vlo[b], t.count(back=2, every=2, unit=16))
                        act.wait_ge(s_vup[b], t.count(back=2, every=2, unit=16))
                    copy(v_own[:, t.i, :], VB[:]).then_inc(s_vown, 1)
                if t := tile(ATT):
                    act.wait_ge(s_tp, t.count(unit=2))
                    need(act, s_o, t.count(back=1))
                    copy(pT[:, 4:8, :], TT[:, 512:1024].rearrange("k (h q) -> k h q", h=4)).then_inc(s_pTa, 1)
                if t := tile(QKV):
                    need(act, s_n2, t.count(back=1))
                    act.wait_ge(s_rot, t.count())
                    nc.scalar.activation(sq[:], QK[:], ACT.Square).then_inc(s_sq, 1)
                if t := tile(TQK):
                    need(act, s_tp, t.count(back=2, unit=2))
                    need(act, s_rsum, t.count(back=2))
                    exponentials(t, 0)
                if t := tile(TH):
                    act.wait_ge(s_th, t.count())
                    if t2 := tile(FFN_IN):
                        act.wait_ge(s_th2, t2.count())
                    need(act, s_v, t.count(back=2))
                    copy(fr(hT[:, t.i % 2, 0, :]), VB[:, 0:P]).then_inc(s_hT, 1)
                if t := tile(FFN_IN):
                    act.wait_ge(s_th2, t.count())
                    copy(fr(h2T[:, 0, t.i * P:t.i * P + P]), VB[:, P:2 * P]).then_inc(s_h2T, 1)
                if t := tile(ATT):
                    act.wait_ge(s_to, t.count())
                    need(act, s_y, t.count(back=1))
                    copy(oT[:], OB[:].rearrange("d (c t) -> d c t", c=PAIRS)).then_inc(s_oT, 1)
                if burst is not None:
                    n = burst
                    for k in range(6):
                        c = k % 3
                        m = CH[c][1]
                        act.wait_ge(s_w1, n * 12 + (2 * k + 1))
                        if k >= 2:
                            act.wait_ge(s_act2, n * 6 + (k - 1))
                        nc.scalar.activation(gelu[0:m, k % 2, :], banks(k)[1][0:m], ACT.Gelu,
                                             bias=b_1[0:m, 3 + c:4 + c]).then_inc(s_gelu, 1)

            act.wait_ge(s_w, N_CONST)
            for l in (1, 0):
                copy(fr(qkv_of[l][0]), qkv_raw[l]).then_inc(s_hi, 1)
                act.wait_ge(s_fold, 1)
                copy(fr(w1_of[l][0]), w_1ln[:, l, :]).then_inc(s_hi, 1)
            act.wait_ge(s_tab, 6 * 16)
            act.wait_ge(s_zero, ZEROED)
            pipeline(act, step, 0)
            stack_done(act, 0)

            with act.Fori(0, SEQS) as s:
                act.wait_ge(g_ty, s + 1)
                copy(y_T, TT[:]).then_inc(g_yT, 1)
                for m, src, dst in ((0, TT, rope_c), (1, SC, rope_s)):
                    act.wait_ge(g_tk, s * 2 + (m + 1))
                    nc.scalar.activation(dst[:], src[:], ACT.Identity, bias=kq_gb[:, 2 * m + 1:2 * m + 2],
                                         scale=kq_gb[:, 2 * m:2 * m + 1]).then_inc(g_kT, 1)
                for i in range(TILES + 1):
                    if i < TILES:
                        b = i % 2
                        act.wait_ge(g_nm, s * TILES + (i + 1))
                        if i >= 2:
                            act.wait_ge(g_tp, s * TILES + (i - 1))
                            act.wait_ge(g_rl, s * TILES + (i - 1))
                        nc.scalar.activation(probs[:, b].rearrange("p a b -> p (a b)"), (QK if b else SC)[:], ACT.Exp,
                                             bias=nm_g[:, b:b + 1], accum_out=sm_g[:, b:b + 1]).then_inc(g_p, 1)
                    if i:
                        k = i - 1
                        b = k % 2
                        act.wait_ge(g_tp, s * TILES + (k + 1))
                        if k >= 2:
                            act.wait_ge(g_o, s * TILES + (k - 1))
                        copy((pT2 if b else pT)[:, 4:8, :],
                             TT[:, 512:1024].rearrange("k (h q) -> k h q", h=4)).then_inc(g_pTa, 1)

            pipeline(act, step, 1)

        @block.gpsimd
        def _(pool):
            g = nc.gpsimd
            pool.wait_ge(s_zero, ZEROED)

            def rstd(slot, lot):
                own = slice(slot, slot + TILES)
                pool.wait_ge(g_mv, lot)
                g.tensor_tensor(ve_g[:, own], mv_g[:, own, 1], epsilon[:, 0:TILES], ALU.add).then_inc(g_ve, 1)
                pool.wait_ge(g_ve, lot)
                g.tensor_tensor(rs_g[:, own], ve_g[:, own], mhalf[:, 0:TILES], ALU.pow).then_inc(g_rs, 1)

            for s in range(SEQS):
                rstd(s * TILES, s + 1)
            pool.wait_ge(s_w, N_CONST)
            for l in range(DEPTH):
                last = g.tensor_scalar(w_1ln[:, l, :], w_1raw[:, l, :], ln_gb_sb[:, 0, l:l + 1], None, ALU.mult)
            last.then_inc(s_fold, 1)

            def step(tile, burst, before):
                if t := tile(FFN_IN):
                    i, b = t.i, t.i % 2
                    need(pool, s_mv2, t.count())
                    g.tensor_tensor(ve2[:, b, :], mv2[:, b, 1:2], epsilon[:, 0:1], ALU.add).then_inc(s_ve2, 1)
                    pool.wait_ge(s_ve2, t.count())
                    g.tensor_tensor(rstd2[:, b, :], ve2[:, b, :], mhalf[:, 0:1], ALU.pow).then_inc(s_rs2, 1)
                    if i == 0:
                        pool.wait_ge(s_ffnw, t.loads() * 96 - 15)
                        k = t.count(back=TILES, every=TILES, unit=2)
                        need(pool, s_xn, k)
                    pool.wait_ge(s_xm, t.count())
                    g.tensor_tensor(x_b2[:, i, :], x_mid[:, i, :], b_2[:], ALU.add).then_inc(s_xb2, 1)
                if t := tile(QKV + 1):
                    b = t.i % 2
                    pool.wait_ge(s_cl, t.count(unit=2) - 1)
                    g.tensor_tensor(rnorm[:, b, :], clip2[:, b, 8:16], mhalf[:, 0:8], ALU.pow).then_inc(s_rn, 1)
                    pool.wait_ge(s_rn, t.count())
                    pool.wait_ge(s_ka, t.count())
                    need(pool, s_tqk, t.count(back=2, unit=2))
                    g.tensor_tensor(k_r[:, b, :].rearrange("p (h d) -> p h d", h=HEADS),
                                    k_a[:].rearrange("p (h d) -> p h d", h=HEADS),
                                    rnorm[:, b, :].unsqueeze(2).to_broadcast([P, HEADS, DH]), ALU.mult).then_inc(s_kr, 1)
                    pool.wait_ge(s_cl, t.count(unit=2))
                    need(pool, s_p, t.count(back=2, unit=2))
                    g.tensor_tensor(qgain[:, b, :], clip2[:, b, 0:8], mhalf[:, 0:8], ALU.pow).then_inc(s_qg, 1)
                if t := tile(QKV):
                    b = t.i % 2
                    pool.wait_ge(s_rot, t.count())
                    need(pool, s_tqk, t.count(back=2, unit=2))
                    g.tensor_tensor(q_r[:, b, :], rope_c[:, 0:512], rope_s[:, 0:512], ALU.add).then_inc(s_qr, 1)
                    need(pool, s_kr, t.count(back=1))
                    g.tensor_tensor(k_a[:], rope_c[:, 512:1024], rope_s[:, 512:1024], ALU.add).then_inc(s_ka, 1)

            pipeline(pool, step, 0)
            stack_done(pool, 0)

            with pool.Fori(0, SEQS) as s:
                rstd(LN_IN, s * 5 + (SEQS + 1))
                pool.wait_ge(g_y, s * 2 + (SEQS + 1))
                g.tensor_tensor(sq[:], flat(x_mid), gelu[:].rearrange("p a b -> p (a b)"), ALU.add).then_inc(g_xy, 1)
                for m in range(3):
                    rstd(KQV + m * TILES, s * 5 + (SEQS + 2 + m))
                pool.wait_ge(g_zn, s * 3 + 3)
                z = act2[:].rearrange("p a b c -> p (a b c)").rearrange("p (i m) -> p i m", i=TILES)
                vz = z[:, :, 2 * DIM:3 * DIM]
                scaled = k_r[:].rearrange("p a (t c) -> p (a t) c", c=DIM)
                g.tensor_tensor(scaled, vz, v_gb[:, 0:1, :].to_broadcast([P, TILES, DIM]), ALU.mult).then_inc(g_vg, 1)
                pool.wait_ge(g_vg, s * 2 + 1)
                g.tensor_tensor(v_g[:], scaled, v_gb[:, 1:2, :].to_broadcast([P, TILES, DIM]), ALU.add).then_inc(g_vg, 1)
                rstd(LN_OUT, s * 5 + (SEQS + 5))

            pipeline(pool, step, 1)


ZEROED = 6
N_CONST = 16 * 16


def tables():
    f = np.float32
    half_idx = np.arange(0, DH, 2, dtype=f)
    inv_freq = (f(1.0) / np.power(f(10000.0), half_idx / f(DH))).astype(f)
    t = np.arange(SLEN, dtype=f)
    ang = (t[:, None] * inv_freq[None, :]).astype(f)
    base = ((half_idx + f(0.4 * DH)) / f(1.4 * DH)).astype(f)
    power = ((t - f(SLEN // 2)) / f(WIN // 2)).astype(f)
    scale = np.power(base[None, :], power[:, None]).astype(f)
    cos, sin = np.cos(ang), np.sin(ang)
    rope = np.zeros((SLEN, 2, 2, DH), f)
    for m, sc in ((0, scale), (1, f(1.0) / scale)):
        rope[:, m, 0, :32] = rope[:, m, 0, 32:] = cos * sc
        rope[:, m, 1, :32] = -sin * sc
        rope[:, m, 1, 32:] = sin * sc
    rope = rope.reshape(TILES, P, 2, 2, DH).transpose(1, 0, 2, 3, 4)
    r = np.arange(WIN)[:, None]
    c = np.arange(WIN)[None, :]
    own, prev = (c <= r), (c >= r)
    allowed = np.zeros((2, P, P), bool)
    allowed[:, :64, :64] = own
    allowed[:, 64:, :64] = prev
    allowed[0, :64, 64:] = prev
    allowed[:, 64:, 64:] = own
    mask = np.where(allowed, 0.0, -1e30).astype(f).transpose(1, 0, 2)
    return (np.ascontiguousarray(rope), np.ascontiguousarray(mask), np.eye(P, dtype=f))


def kernel(**inputs):
    import concourse.bacc as bacc
    from concourse.bass_utils import run_bass_kernel_spmd

    a = {k: np.asarray(v) for k, v in inputs.items()}
    A, L = "L0_attn_", "L0_ffn_"
    rope, mask, ident = tables()
    b1 = np.zeros((DEPTH, 2, 3 * P), a[L + "b1"].dtype)
    b1[:, :, :HID] = a[L + "b1"].reshape(DEPTH, 2, HID)
    b1 = b1.reshape(DEPTH, 6, P).transpose(2, 0, 1)
    arrays = {
        "x_in": a[A + "input_sequence"],
        "w_attn": np.stack([a[A + "Wk"], a[A + "Wq"], a[A + "Wv"]], axis=1),
        "b_attn": np.concatenate([a[A + "bk"], a[A + "bq"], a[A + "bv"]]),
        "kq_gain": np.stack([a[A + "gk"], a[A + "betak"], a[A + "gq"], a[A + "betaq"]], axis=1),
        "v_gain": np.stack([a[A + "gv"], a[A + "betav"]]),
        "wqkv": a[L + "wqkv"],
        "qk_gain": np.stack([a[L + "q_scale"], a[L + "k_scale"]], axis=1),
        "wo_in": a[L + "wo"],
        "ln_gb": np.stack([a[L + "ln_g"].T, a[L + "ln_b"].T], axis=1),
        "w1_in": a[L + "w1"], "b1_in": b1, "w2_in": a[L + "w2"], "b2_in": a[L + "b2"],
        "rope_in": rope, "mask_in": mask, "ident_in": ident,
    }
    arrays = {k: np.ascontiguousarray(v) for k, v in arrays.items()}
    nc = bacc.Bacc("TRN2", target_bir_lowering=False, num_devices=1)
    args = [nc.dram_tensor(k, v.shape, mybir.dt.from_np(v.dtype), kind="ExternalInput").ap() for k, v in arrays.items()]
    out = nc.dram_tensor("out", [SEQS, SLEN, DIM], F32, kind="ExternalOutput").ap()
    build(nc, *args, out)
    r = run_bass_kernel_spmd(nc, [arrays], core_ids=[0])
    return r.results[0]["out"]
```
